# Optimizing a Trainium2 kernel written in Bass

```python
import numpy as np
import jax
import jax.numpy as jnp

def _softmax(x, axis=-1):
    return jax.nn.softmax(x, axis=axis)

def _gelu(x):
    return jax.nn.gelu(x, approximate=True)

def _silu(x):
    return jax.nn.silu(x)

def _sigmoid(x):
    return jax.nn.sigmoid(x)

def _layernorm(x, axis=-1, eps=1e-05):
    m = jnp.mean(x, axis=axis, keepdims=True)
    v = jnp.var(x, axis=axis, keepdims=True)
    return (x - m) / jnp.sqrt(v + eps)

def _scatter_add(tgt, idx, src, axis=0):
    return tgt.at[idx].add(src)

def _segment_sum(src, seg, n):
    return jax.ops.segment_sum(src, seg, n)
kernel_name = 'mk_adj_resnorm_d2_adj_r2_0a8c50'

def setup_inputs(seed: int=0):
    np.random.seed(seed)
    _w = jnp.asarray

    def _rec_inputs():
        import jax
        import jax.numpy as jnp
        _gk = jax.random.key(seed)
        x = -0.0003482 + 1 * jax.random.normal(jax.random.fold_in(_gk, 1), (8, 1024, 512), jnp.float32)
        _a = jax.random.bernoulli(jax.random.fold_in(_gk, 2), 0.00390625, (8, 1024, 1024))
        _a = jnp.logical_or(_a, jnp.swapaxes(_a, -1, -2))
        _a = jnp.logical_or(_a, jnp.eye(1024, dtype=bool))
        _af = _a.astype(jnp.float32)
        _af = _af * jax.random.uniform(jax.random.fold_in(_gk, 3), (8, 1024, 1024), jnp.float32, 0.05, 0.999837)
        adj = _af
        return (x, adj)
    x, adj = _rec_inputs()

    def _L0_gnn_setup():
        import jax, jax.numpy as jnp
        import numpy as np
        B, K, D = (256, 36, 512)
        N_KERNELS = 4
        OUT_DIM = 512
        OUT_PER_KERNEL = OUT_DIM // N_KERNELS
        key = jax.random.key(seed)
        k1, k2, k3, k4, k5 = jax.random.split(key, 5)
        neighbourhood_features = jax.random.normal(k1, (B, K, D), dtype=jnp.float32)
        region_relation_weights = jax.random.uniform(k2, (B, K, K), dtype=jnp.float32)
        mean_relation = jax.random.uniform(k3, (N_KERNELS,), dtype=jnp.float32)
        precision_relation = jax.random.uniform(k4, (N_KERNELS,), dtype=jnp.float32)
        bound = 1.0 / np.sqrt(D)
        W = jax.random.uniform(k5, (N_KERNELS, OUT_PER_KERNEL, D), dtype=jnp.float32, minval=-bound, maxval=bound)
        return {'neighbourhood_features': neighbourhood_features, 'region_relation_weights': region_relation_weights, 'mean_relation': mean_relation, 'precision_relation': precision_relation, 'W': W}
    _L0_gnn_all = _L0_gnn_setup()
    _L0_gnn_in = {k: v for k, v in _L0_gnn_all.items() if k in ('mean_relation', 'precision_relation', 'W')}
    del _L0_gnn_all

    def _L1_gnn_setup():
        import jax, jax.numpy as jnp
        import numpy as np
        B, N, H, E = (64, 256, 512, 4)
        BN_EPS = 1e-05
        key = jax.random.key(seed)
        ks = jax.random.split(key, 6)
        x = jax.random.normal(ks[0], (B, N, H), dtype=jnp.float32)
        adj = jax.random.uniform(ks[1], (B, N, N), dtype=jnp.float32)
        stdv = 1.0 / np.sqrt(H)
        expert_w = jax.random.uniform(ks[2], (E, H, H), minval=-stdv, maxval=stdv, dtype=jnp.float32)
        r_std = 1.0 / np.sqrt(H)
        router_w = jax.random.uniform(ks[3], (H, E), minval=-r_std, maxval=r_std, dtype=jnp.float32)
        router_b = jax.random.uniform(ks[4], (E,), minval=-r_std, maxval=r_std, dtype=jnp.float32)
        bn_gamma = jnp.ones((E, H), dtype=jnp.float32)
        bn_beta = jnp.zeros((E, H), dtype=jnp.float32)
        return {'x': x, 'adj': adj, 'router_w': router_w, 'router_b': router_b, 'expert_w': expert_w, 'bn_gamma': bn_gamma, 'bn_beta': bn_beta}
    _L1_gnn_all = _L1_gnn_setup()
    _L1_gnn_in = {k: v for k, v in _L1_gnn_all.items() if k in ('router_w', 'router_b', 'expert_w', 'bn_gamma', 'bn_beta')}
    del _L1_gnn_all
    return {'x': x, 'adj': adj, 'L0_gnn_mean_relation': _L0_gnn_in['mean_relation'], 'L0_gnn_precision_relation': _L0_gnn_in['precision_relation'], 'L0_gnn_W': _L0_gnn_in['W'], 'L1_gnn_router_w': _L1_gnn_in['router_w'], 'L1_gnn_router_b': _L1_gnn_in['router_b'], 'L1_gnn_expert_w': _L1_gnn_in['expert_w'], 'L1_gnn_bn_gamma': _L1_gnn_in['bn_gamma'], 'L1_gnn_bn_beta': _L1_gnn_in['bn_beta']}

def reference(x, adj, L0_gnn_mean_relation, L0_gnn_precision_relation, L0_gnn_W, L1_gnn_router_w, L1_gnn_router_b, L1_gnn_expert_w, L1_gnn_bn_gamma, L1_gnn_bn_beta):
    import jax
    import jax.numpy as jnp

    def _L0_gnn_ref(neighbourhood_features, region_relation_weights, mean_relation, precision_relation, W):
        import jax, jax.numpy as jnp
        import numpy as np
        B, K, D = (256, 36, 512)
        N_KERNELS = 4
        OUT_DIM = 512
        OUT_PER_KERNEL = OUT_DIM // N_KERNELS
        b, k, d = neighbourhood_features.shape
        diff = (region_relation_weights[..., None] - mean_relation) ** 2
        w = jnp.exp(-0.5 * diff / (1e-14 + precision_relation ** 2))
        w = w / jnp.sum(w, axis=-1, keepdims=True)
        ws = jnp.sum(w, axis=2)
        weighted = ws[..., None] * neighbourhood_features[:, :, None, :]
        out = jnp.einsum('bknd,nod->bkno', weighted, W)
        return out.reshape(b, k, -1)

    def _L1_gnn_ref(x, adj, router_w, router_b, expert_w, bn_gamma, bn_beta):
        import jax, jax.numpy as jnp
        import numpy as np
        B, N, H, E = (64, 256, 512, 4)
        BN_EPS = 1e-05
        scores = x.mean(axis=1) @ router_w + router_b
        top1 = jnp.argmax(scores, axis=-1)
        n_exp = expert_w.shape[0]
        W = expert_w[top1]
        support = jnp.einsum('bnh,bhk->bnk', x, W)
        out = jnp.einsum('bnm,bmk->bnk', adj, support)
        s = jax.ops.segment_sum(out.sum(axis=1), top1, num_segments=n_exp)
        ss = jax.ops.segment_sum((out * out).sum(axis=1), top1, num_segments=n_exp)
        cnt = jax.ops.segment_sum(jnp.ones_like(top1, dtype=out.dtype), top1, num_segments=n_exp) * out.shape[1]
        cnt = jnp.maximum(cnt, 1.0)[:, None]
        mean = s / cnt
        var = ss / cnt - mean * mean
        m = mean[top1][:, None, :]
        inv = jax.lax.rsqrt(var[top1][:, None, :] + BN_EPS)
        y = (out - m) * inv * bn_gamma[top1][:, None, :] + bn_beta[top1][:, None, :]
        return jax.nn.relu(y)
    x = _layernorm(x + _L0_gnn_ref(x, adj, L0_gnn_mean_relation, L0_gnn_precision_relation, L0_gnn_W), axis=-1)
    x = _layernorm(x + _L1_gnn_ref(x, adj, L1_gnn_router_w, L1_gnn_router_b, L1_gnn_expert_w, L1_gnn_bn_gamma, L1_gnn_bn_beta), axis=-1)
    return x

_drawn_inputs = setup_inputs


def setup_inputs(seed=0):
    import zlib

    import numpy as np

    out = dict(_drawn_inputs(seed))
    spreads = {'L1_gnn_bn_gamma': (1.0, 0.2), 'L1_gnn_bn_beta': (0.0, 0.1)}
    factors = {}
    for name, (base, spread) in spreads.items():
        noise = np.random.default_rng([zlib.crc32(name.encode()), seed]).standard_normal(out[name].shape)
        drawn = base * np.exp(spread * noise) if base else spread * noise
        out[name] = jnp.asarray(drawn.astype(out[name].dtype))
    for name, factor in factors.items():
        out[name] = (out[name] * factor).astype(out[name].dtype)
    return out
```

```python
from contextlib import ExitStack

import concourse.bass as bass
from concourse import mybir

ALU = mybir.AluOpType
ACT = mybir.ActivationFunctionType
F32 = mybir.dt.float32
I32 = mybir.dt.int32
AX_X = mybir.AxisListType.X

P = 128
LN_EPS = 1e-5
BN_EPS = 1e-5
SUM_SCALE = 2.0 ** 60
SPAN = 16
B_LAG = 9
C_LAG = 13


class Slot:

    def __init__(self, p, r, total):
        self.p, self.r, self.total = p, r, total
        self.fixed = isinstance(p, int)

    def live(self, lag=0):
        return not self.fixed or 0 <= SPAN * self.p + self.r - lag < self.total

    def mod(self, m, lag=0):
        return (self.r - lag) % m

    def div(self, m, lag=0):
        return self.p * (SPAN // m) + (self.r - lag) // m

    def count(self, per=1, plus=0, lag=0):
        return self.p * (SPAN * per) + (per * (self.r - lag) + plus)


def wait(eng, sem, value):
    if isinstance(value, int) and value <= 0:
        return
    eng.wait_ge(sem, value)


def held(eng, value):
    return value if isinstance(value, int) else eng.to_reg(value)


def gnn_program(nc, x, adj, mean_rel, prec_rel, w0, router_w, router_b, expert_w, gamma, beta, x1_spill,
                out_spill, out):
    NB, NR, D = x.shape
    NK = mean_rel.shape[0]
    E = expert_w.shape[0]
    T = NR // P
    C = D // P
    G = 4
    HALF = NR // 2
    TILES = NB * T
    KW = D // NK
    assert T == 8 and C == 4 and NK == 4 and HALF == 512 and KW == P and TILES % SPAN == 0

    with ExitStack() as ctx:
        def sb(name, shape, dt=F32):
            return ctx.enter_context(nc.sbuf_tensor(name, shape, dt))

        def sem(name):
            return ctx.enter_context(nc.semaphore(name))

        def sems(name, n):
            return [sem(f"{name}{i}") for i in range(n)]

        adj_in = sb("adj_in", [P, 2, NR])
        x_in = sb("x_in", [P, 4, D])
        adjT = sb("adjT", [P, 2, T, NR])
        x1 = sb("x1", [P, 2, T, D])
        w_sel = sb("w_sel", [P, 2, C, D])
        w0T = sb("w0T", [P, C, D])
        xT = sb("xT", [P, 2, C, P])
        wgt = sb("wgt", [P, 2, NK, NR])
        tot = sb("tot", [P, 2, NR])
        zT = sb("zT", [P, 2, C, HALF])
        o_stage = sb("o_stage", [P, 4, HALF])
        ident = sb("ident", [P, P])
        ones = sb("ones", [P, P])
        neg_mu = sb("neg_mu", [P, NK])
        neg_alpha = sb("neg_alpha", [P, NK])
        eps = sb("eps", [P, 1])
        wsum = sb("wsum", [P, 2, NK])
        y_stat = sb("y_stat", [P, 2, 6])
        y_mv = sb("y_mv", [P, 2, G, 2])
        ln_var = sb("ln_var", [P, G])
        rstd = sb("rstd", [P, 2, G])
        nmr = sb("nmr", [P, 2, G])
        o_stat = sb("o_stat", [P, 2, C, 2, 6])
        o_agg = sb("o_agg", [P, C, 2])
        pad = sb("pad", [P, 1])
        o_mv = sb("o_mv", [P, NB, C, 2])
        rw = sb("rw", [P, C, E])
        rb = sb("rb", [1, E])
        iota_f = sb("iota_f", [1, E])
        iota_i = sb("iota_i", [1, E], I32)
        meanT = sb("meanT", [P, C])
        sc = sb("sc", [1, E])
        sc_max = sb("sc_max", [1, 1])
        sc_idx = sb("sc_idx", [1, 1])
        sc_int = sb("sc_int", [1, 2], I32)
        hot_row = sb("hot_row", [1, NB, E])
        hot = sb("hot", [P, NB, E])
        gamT = sb("gamT", [P, E, C])
        betT = sb("betT", [P, E, C])
        e_sum = sb("e_sum", [P, E, 2 * C])
        e_cnt = sb("e_cnt", [P, E])
        e_sq = sb("e_sq", [P, E, C])
        e_lnv = sb("e_lnv", [P, E, C])
        e_scale = sb("e_scale", [P, E, C])
        e_bias = sb("e_bias", [P, E, C])
        b_scale = sb("b_scale", [P, NB, C])
        b_bias = sb("b_bias", [P, NB, C])

        ps_adjT = ctx.enter_context(nc.psum_tensor("ps_adjT", [P, 2, 512], F32))
        ps_xT = ctx.enter_context(nc.psum_tensor("ps_xT", [P, 512], F32))
        ps_h = ctx.enter_context(nc.psum_tensor("ps_h", [P, 512], F32))
        ps_z = ctx.enter_context(nc.psum_tensor("ps_z", [P, 2, 512], F32))
        ps_o = ctx.enter_context(nc.psum_tensor("ps_o", [P, 512], F32))
        ps_s = ctx.enter_context(nc.psum_tensor("ps_s", [P, 512], F32))

        adj_landed = sems("adj_landed", 2)
        x_landed = sems("x_landed", 4)
        w_landed = sems("w_landed", 2)
        o_stored = sems("o_stored", 4)
        x1_stored = sems("x1_stored", 4)
        const_landed = sem("const_landed")
        w0_landed = sem("w0_landed")
        bn_landed = sem("bn_landed")
        pe_adjT, pe_xT, pe_h, pe_z, pe_o = (sem(f"pe_{k}") for k in ("adjT", "xT", "h", "z", "o"))
        pe_mean, pe_score, pe_w0, pe_hot, pe_back = (sem(f"pe_{k}") for k in ("mean", "score", "w0", "hot", "back"))
        act_sq, act_w, act_adjT, act_xT = (sem(f"act_{k}") for k in ("sq", "w", "adjT", "xT"))
        act_ln, act_rec, act_z, act_o = (sem(f"act_{k}") for k in ("ln", "rec", "z", "o"))
        act_lnv, act_rstd, act_bn, act_relu = (sem(f"act_{k}") for k in ("lnv", "rstd", "bn", "relu"))
        act_lnv2, act_rstd2, act_out = (sem(f"act_{k}") for k in ("lnv2", "rstd2", "out"))
        dve_tot, dve_ws, dve_y, dve_stat, dve_mv = (sem(f"dve_{k}") for k in ("tot", "ws", "y", "stat", "mv"))
        dve_x1, dve_ostat, dve_omv, dve_meanT = (sem(f"dve_{k}") for k in ("x1", "ostat", "omv", "meanT"))
        dve_routing, dve_oagg = sem("dve_routing"), sem("dve_oagg")
        dve_route, dve_const, dve_w0, dve_bn = (sem(f"dve_{k}") for k in ("route", "const", "w0", "bn"))
        dve_y2, dve_stat2, dve_mv2, dve_nmr2 = (sem(f"dve_{k}") for k in ("y2", "stat2", "mv2", "nmr2"))
        pool_const = sem("pool_const")
        o_back, x1_back, y_stored = sems("o_back", 4), sems("x1_back", 4), sems("y_stored", 4)

        adjT_flat = adjT[:].rearrange("p a t n -> p (a t n)")
        wgt_flat = wgt[:].rearrange("p a k n -> p (a k n)")
        x1_flat = x1[:].rearrange("p a t n -> p (a t n)")
        bn_a = tot[:, 0, 0:2 * NB * C * E]
        BUF = T * D
        areas = [adjT_flat[:, 0:BUF], adjT_flat[:, BUF:2 * BUF], wgt_flat[:, 0:BUF], wgt_flat[:, BUF:2 * BUF],
                 adjT_flat[:, 2 * BUF:3 * BUF], adjT_flat[:, 3 * BUF:4 * BUF], x1_flat[:, 0:BUF],
                 x1_flat[:, BUF:2 * BUF]]
        o_buf = [areas[2 * i].rearrange("p (c n) -> p c n", c=C) for i in range(4)]
        y_buf = [areas[2 * i + 1].rearrange("p (t n) -> p t n", t=T) for i in range(4)]
        ps_y = [ps_adjT[:, 0, :], ps_adjT[:, 1, :], ps_xT[:], ps_h[:]]

        PAIRS = TILES // SPAN
        LAST = TILES + C_LAG + 1

        def run_slots(eng, body):
            for r in range(SPAN):
                body(Slot(0, r, TILES))
            with eng.Fori(1, PAIRS) as p:
                for r in range(SPAN):
                    body(Slot(p, r, TILES))
            for n in range(TILES, LAST):
                body(Slot(PAIRS, n - TILES, TILES))

        def run_batches(eng, body):
            for i in range(4):
                body(0, i)
            with eng.Fori(1, NB // 4) as q:
                for i in range(4):
                    body(q, i)

        BN_VAR, BN_DONE = 10, 17

        block = ctx.enter_context(nc.Block())

        @block.sync
        def _(sp):
            sp.dma_start(neg_mu[:], mean_rel.rearrange("(o k) -> o k", o=1).broadcast_to([P, NK])).then_inc(const_landed, 16)
            sp.dma_start(neg_alpha[:], prec_rel.rearrange("(o k) -> o k", o=1).broadcast_to([P, NK])).then_inc(const_landed, 16)

            def load_adj(s, ahead):
                squared = held(sp, s.count(4, plus=4 * (ahead - 1)))
                transposed = held(sp, s.count(2, plus=2 * (ahead - 1)))
                wait(sp, act_sq, squared)
                wait(sp, pe_adjT, transposed)
                k = s.mod(2, -ahead)
                src = adj.rearrange("b (t p) n -> (b t) p n", p=P)[s.count(1, plus=ahead)]
                sp.dma_start(adj_in[:, k, :], src).then_inc(adj_landed[k], 16)

            def load_x(s, ahead):
                wait(sp, dve_y, s.count(1, plus=ahead - 3))
                k = s.mod(4, -ahead)
                src = x.rearrange("b (t p) n -> (b t) p n", p=P)[s.count(1, plus=ahead)]
                sp.dma_start(x_in[:, k, :], src).then_inc(x_landed[k], 16)

            for k in range(2):
                sp.dma_start(adj_in[:, k, :], adj[0, k * P:(k + 1) * P, :]).then_inc(adj_landed[k], 16)
                sp.dma_start(x_in[:, k, :], x[0, k * P:(k + 1) * P, :]).then_inc(x_landed[k], 16)
                if k == 0:
                    sp.dma_start(wgt[:, 1, :, 0:D], w0.rearrange("n o d -> o n d")).then_inc(w0_landed, 16)
            sp.dma_start(rw[:], router_w.rearrange("(c p) e -> p c e", p=P)).then_inc(const_landed, 16)
            sp.dma_start(rb[:], router_b.rearrange("(o e) -> o e", o=1)).then_inc(const_landed, 16)

            def body(s):
                routed = s.mod(T) == 4 and s.live(T)
                if routed:
                    route_count, unit_count = held(sp, s.div(T)), held(sp, s.count(1, plus=-2 * T - 4))
                    wait(sp, dve_route, route_count)
                    wait(sp, pe_o, unit_count)
                if s.live(-2):
                    load_x(s, 2)
                    load_adj(s, 2)
                if routed:
                    m = s.mod(2 * T, T) // T
                    e = sp.value_load(sc_int[0:1, m:m + 1], min_val=0, max_val=E - 1)
                    sp.dma_start(w_sel[:, m, :, :],
                                 expert_w.rearrange("e (c p) k -> e p c k", p=P)[e]).then_inc(w_landed[m], 16)

            for r in range(SPAN):
                body(Slot(0, r, TILES))
            with sp.Fori(1, PAIRS - 1) as p:
                for r in range(SPAN):
                    body(Slot(p, r, TILES))
            for n in range(TILES - SPAN, LAST):
                body(Slot(n // SPAN, n % SPAN, TILES))

            def back(q, i):
                b = q * 4 + i
                if isinstance(q, int) and q == 0:
                    if i == 0:
                        sp.wait_ge(pe_z, TILES - T)
                    elif i == 1:
                        sp.wait_ge(dve_ws, TILES)
                    else:
                        sp.wait_ge(pe_z, TILES)
                    if i == 3:
                        for k in range(4):
                            sp.wait_ge(x1_stored[k], 16 * TILES // G // 4)
                else:
                    sp.wait_ge(y_stored[i], q * 32)
                    sp.wait_ge(o_back[i], q * 16)
                    sp.wait_ge(x1_back[i], q * 16)
                for k in range(4):
                    sp.wait_ge(o_stored[k], q * 128 + (i + 1) * 32)
                for k in range(2):
                    sp.wait_ge(x1_stored[(2 * i + k) % 4], q * 32 + (i // 2 + 1) * 16)
                sp.dma_start(o_buf[i], out_spill.rearrange("b (c p) n -> b p c n", p=P)[b]).then_inc(o_back[i], 16)
                sp.dma_start(y_buf[i], x1_spill.rearrange("b (t p) n -> b p t n", p=P)[b]).then_inc(x1_back[i], 16)

            for i in range(4):
                back(0, i)
            with sp.Fori(1, NB // 4) as q:
                for i in range(4):
                    back(q, i)

        @block.gpsimd
        def _(pool):
            nc.gpsimd.memset(ident[:], 0.0).then_inc(pool_const, 1)
            pool.wait_ge(pool_const, 1)
            nc.gpsimd.affine_select(out=ident[:], in_=ident[:], compare_op=ALU.not_equal, fill=1.0, base=0,
                                    pattern=[[-1, P]], channel_multiplier=1).then_inc(pool_const, 1)
            nc.gpsimd.iota(iota_i[:], pattern=[[1, E]], base=0, channel_multiplier=0).then_inc(pool_const, 1)
            with nc.allow_non_contiguous_dma("two small transposed tables"):
                for k in range(C):
                    pool.dma_start(gamT[:, :, k], gamma[:, k * P:(k + 1) * P].rearrange("e p -> p e")).then_inc(bn_landed, 16)
                    pool.dma_start(betT[:, :, k], beta[:, k * P:(k + 1) * P].rearrange("e p -> p e")).then_inc(bn_landed, 16)

            def body(s):
                if s.mod(G) == 1 and s.live(G + 1):
                    pool.wait_ge(dve_x1, s.count(1, lag=1))
                    g = s.mod(SPAN, G + 1) // G
                    h, m = g % 2, g // 2
                    dst = x1_spill.rearrange("b (g t p) n -> (b g) p t n", g=2, p=P)[s.div(G, G + 1)]
                    pool.dma_start(dst, x1[:, m, h * G:(h + 1) * G, :]).then_inc(x1_stored[g], 16)
                if s.live(C_LAG + 1):
                    pool.wait_ge(act_o, s.count(1, plus=1, lag=C_LAG + 1))
                    k = s.mod(4, C_LAG + 1)
                    half = s.mod(T, C_LAG + 1) // 4
                    dst = out_spill.rearrange("b (c p) n -> b c p n", p=P)[
                        s.div(T, C_LAG + 1), k, :, half * HALF:(half + 1) * HALF]
                    pool.dma_start(dst, o_stage[:, k, :]).then_inc(o_stored[k], 16)

            run_slots(pool, body)

            def out_rows(q, i):
                for g in range(2):
                    pool.wait_ge(act_out, q * (4 * T) + i * T + (g + 1) * G)
                    dst = out.rearrange("b (g t p) n -> b g p t n", g=2, p=P)[q * 4 + i, g]
                    pool.dma_start(dst, y_buf[i][:, g * G:(g + 1) * G, :]).then_inc(y_stored[i], 16)

            run_batches(pool, out_rows)
            for i in range(4):
                pool.wait_ge(y_stored[i], NB // 4 * 32)

        @block.scalar
        def _(act):
            nc.scalar.preload_act_table_set("natural_log_exp_and_others")
            act.wait_ge(dve_const, 3)

            def body(s):
                if s.live(B_LAG + 1):
                    u, half, k = s.mod(2, B_LAG + 1), s.mod(T, B_LAG + 1) // 4, s.mod(4, B_LAG + 1)
                    act.wait_ge(pe_z, s.count(1, plus=1, lag=B_LAG + 1))
                    if k == 0:
                        wait(act, pe_o, s.count(1, plus=-4, lag=B_LAG + 1))
                    nc.scalar.activation(zT[:, half, k, :], ps_z[:, u, :], ACT.Copy).then_inc(act_z, 1)
                if s.live(C_LAG + 1):
                    k = s.mod(4, C_LAG + 1)
                    act.wait_ge(pe_o, s.count(1, plus=1, lag=C_LAG + 1))
                    wait(act, o_stored[k], s.div(4, C_LAG + 1) * 16)
                    wait(act, dve_ostat, s.count(1, plus=-1, lag=C_LAG + 1))
                    nc.scalar.activation(o_stage[:, k, :], ps_o[:], ACT.Copy).then_inc(act_o, 1)
                if s.live():
                    a, m = s.mod(2), s.mod(2)
                    act.wait_ge(adj_landed[a], s.div(2) * 16 + 16)
                    wait(act, dve_ws, s.count(1, plus=-1))
                    if s.fixed and s.p == 0 and s.r == 1:
                        act.wait_ge(pe_w0, C)
                    for k in range(NK):
                        nc.scalar.activation(wgt[:, m, k, :], adj_in[:, a, :], ACT.Square,
                                             bias=neg_mu[:, k:k + 1]).then_inc(act_sq, 1)
                    act.wait_ge(pe_xT, s.count(1, plus=1))
                    wait(act, pe_h, s.count(1, plus=-1))
                    nc.scalar.activation(xT[:, m, :, :].rearrange("p c n -> p (c n)"), ps_xT[:],
                                         ACT.Copy).then_inc(act_xT, 1)
                    for k in range(NK):
                        act.wait_ge(act_sq, s.count(4, plus=k + 1))
                        nc.scalar.activation(wgt[:, m, k, :], wgt[:, m, k, :], ACT.Exp,
                                             scale=neg_alpha[:, k:k + 1]).then_inc(act_w, 1)
                    b, t = s.mod(2 * T) // T, s.mod(T)
                    if t % 4 == 0:
                        wait(act, pe_z, s.count(1, plus=-12))
                    for h in range(2):
                        act.wait_ge(pe_adjT, s.count(2, plus=h + 1))
                        nc.scalar.activation(adjT[:, b, 4 * h:4 * h + 4, t * P:(t + 1) * P],
                                             ps_adjT[:, h, :].rearrange("p (c n) -> p c n", c=4),
                                             ACT.Copy).then_inc(act_adjT, 1)
                if s.mod(G) == 0 and s.live(G):
                    g = s.mod(2 * G, G) // G
                    act.wait_ge(dve_mv, s.count(1))
                    nc.scalar.activation(ln_var[:], y_mv[:, g, :, 1], ACT.Ln, bias=eps[:, 0:1]).then_inc(act_lnv, 1)
                    act.wait_ge(act_lnv, s.div(G))
                    nc.scalar.activation(rstd[:, g, :], ln_var[:], ACT.Exp, scale=-0.5).then_inc(act_rstd, 1)
                if s.live():
                    act.wait_ge(dve_tot, s.count(3, plus=3))
                    nc.scalar.activation(tot[:, m, :], tot[:, m, :], ACT.Ln, scale=SUM_SCALE).then_inc(act_ln, 1)
                    act.wait_ge(act_ln, s.count(1, plus=1))
                    nc.scalar.activation(tot[:, m, :], tot[:, m, :], ACT.Exp, scale=-1.0).then_inc(act_rec, 1)

            run_slots(act, body)

            act.wait_ge(dve_bn, BN_VAR)
            nc.scalar.activation(e_lnv[:], e_sq[:], ACT.Ln, bias=eps[:, 0:1]).then_inc(act_bn, 1)
            act.wait_ge(act_bn, 1)
            nc.scalar.activation(e_scale[:], e_lnv[:], ACT.Exp, scale=-0.5).then_inc(act_bn, 1)
            act.wait_ge(dve_bn, BN_DONE)

            def rows(q, i):
                act.wait_ge(o_back[i], q * 16 + 16)
                for k in range(C):
                    nc.scalar.activation(o_buf[i][:, k, :], o_buf[i][:, k, :], ACT.Relu,
                                         bias=q_bias(q, i, k), scale=q_scale(q, i, k)).then_inc(act_relu, 1)
                for g in range(2):
                    done = q * (4 * T) + (i * T + g * G)
                    groups = q * 8 + (i * 2 + g)
                    act.wait_ge(dve_mv2, done + G)
                    nc.scalar.activation(ln_var[:], y_mv[:, g, :, 1], ACT.Ln, bias=eps[:, 0:1]).then_inc(act_lnv2, 1)
                    act.wait_ge(act_lnv2, groups + 1)
                    nc.scalar.activation(rstd[:, g, :], ln_var[:], ACT.Exp, scale=-0.5).then_inc(act_rstd2, 1)
                    act.wait_ge(act_rstd2, groups + 1)
                    act.wait_ge(dve_nmr2, groups + 1)
                    for t in range(G):
                        row = y_buf[i][:, g * G + t, :]
                        nc.scalar.activation(row, row, ACT.Identity, bias=nmr[:, g, t:t + 1],
                                             scale=rstd[:, g, t:t + 1]).then_inc(act_out, 1)

            def q_scale(q, i, k):
                return b_scale[:].rearrange("p b c -> p (b c)")[:, bass.ds(q * (4 * C) + (i * C + k), 1)]

            def q_bias(q, i, k):
                return b_bias[:].rearrange("p b c -> p (b c)")[:, bass.ds(q * (4 * C) + (i * C + k), 1)]

            run_batches(act, rows)


        @block.vector
        def _(dve):
            v = nc.vector
            v.memset(ones[:], 1.0).then_inc(dve_const, 1)
            v.memset(eps[:], LN_EPS)
            dve.wait_ge(const_landed, 64)
            v.tensor_tensor(neg_alpha[:], neg_alpha[:], neg_alpha[:], ALU.mult).then_inc(dve_w0, 1)
            dve.wait_ge(dve_w0, 1)
            v.tensor_scalar(neg_alpha[:], neg_alpha[:], 1e-14, -2.0, ALU.add, ALU.mult).then_inc(dve_w0, 1)
            dve.wait_ge(dve_w0, 2)
            v.reciprocal(neg_alpha[:], neg_alpha[:]).then_inc(dve_const, 1)
            v.tensor_scalar(neg_mu[:], neg_mu[:], -1.0, None, ALU.mult).then_inc(dve_const, 1)
            dve.wait_ge(pool_const, 3)
            v.tensor_copy(iota_f[:], iota_i[:]).then_inc(dve_const, 1)
            for c in range(C):
                dve.wait_ge(pe_w0, c + 1)
                v.tensor_copy(w0T[:, c, :], ps_adjT[:, c % 2, :]).then_inc(dve_w0, 1)

            def body(s):
                if s.live(C_LAG + 1):
                    half, k = s.mod(T, C_LAG + 1) // 4, s.mod(4, C_LAG + 1)
                    m = s.mod(2 * T, C_LAG + 1) // T
                    dve.wait_ge(act_o, s.count(1, plus=1, lag=C_LAG + 1))
                    v.bn_stats(o_stat[:, m, k, half, :], o_stage[:, k, :]).then_inc(dve_ostat, 1)
                    if half == 1 and k == 3:
                        dve.wait_ge(dve_ostat, s.count(1, plus=1, lag=C_LAG + 1))
                        v.memset(pad[:], 0.0)
                        for c in range(C):
                            last = v.bn_aggr(o_agg[:, c, :], o_stat[:, m, c, :, :].rearrange("p h s -> p (h s)"))
                        last.then_inc(dve_oagg, 1)
                        dve.wait_ge(dve_oagg, s.div(T, C_LAG + 1) + 1)
                        v.tensor_copy(o_mv[:].rearrange("p b c s -> p (b c s)")[
                            :, bass.ds(s.div(T, C_LAG + 1) * (2 * C), 2 * C)],
                            o_agg[:].rearrange("p c s -> p (c s)")).then_inc(dve_omv, 1)
                if s.live(1):
                    j, t, m = s.mod(2, 1), s.mod(T, 1), s.mod(2 * T, 1) // T
                    dve.wait_ge(act_rec, s.count(1))
                    for k in range(NK):
                        v_ws = v.scalar_tensor_tensor(out=wgt[:, j, k, :], in0=wgt[:, j, k, :], scalar=SUM_SCALE,
                                                      in1=tot[:, j, :], op0=ALU.mult, op1=ALU.mult,
                                                      accum_out=wsum[:, j, k:k + 1])
                    v_ws.then_inc(dve_ws, 1)
                    dve.wait_ge(dve_ws, s.count(1))
                    dve.wait_ge(pe_h, s.count(1))
                    dve.wait_ge(x_landed[s.mod(4, 1)], s.div(4, 1) * 16 + 16)
                    if t == 0:
                        wait(dve, pe_z, s.count(1, plus=-T, lag=1))
                    if t % G == 0:
                        wait(dve, x1_stored[s.mod(SPAN, 1) // G], s.div(SPAN, 1) * 16)
                    for k in range(NK):
                        f = slice(k * KW, (k + 1) * KW)
                        v_y = v.scalar_tensor_tensor(out=x1[:, m, t, f], in0=ps_h[:, f], scalar=wsum[:, j, k:k + 1],
                                                     in1=x_in[:, s.mod(4, 1), f], op0=ALU.mult, op1=ALU.add)
                    v_y.then_inc(dve_y, 1)
                    dve.wait_ge(dve_y, s.count(1))
                    v.bn_stats(y_stat[:, j, :], x1[:, m, t, :]).then_inc(dve_stat, 1)
                if s.live():
                    m = s.mod(2)
                    wait(dve, dve_stat, s.count(1))
                    dve.wait_ge(act_w, s.count(4, plus=2))
                    v.tensor_tensor(tot[:, m, :], wgt[:, m, 0, :], wgt[:, m, 1, :], ALU.add).then_inc(dve_tot, 1)
                    for k in range(2, NK):
                        dve.wait_ge(act_w, s.count(4, plus=k + 1))
                        dve.wait_ge(dve_tot, s.count(3, plus=k - 1))
                        v.tensor_tensor(tot[:, m, :], tot[:, m, :], wgt[:, m, k, :], ALU.add).then_inc(dve_tot, 1)
                if s.live(1):
                    g, tg = s.mod(2 * G, 1) // G, s.mod(G, 1)
                    if not s.live():
                        dve.wait_ge(dve_stat, s.count(1))
                    v.bn_aggr(y_mv[:, g, tg, :], y_stat[:, s.mod(2, 1), :]).then_inc(dve_mv, 1)
                if s.mod(G) == 0 and s.live(G):
                    g, h, m = s.mod(2 * G, G) // G, s.mod(T, G) // G, s.mod(2 * T, G) // T
                    dve.wait_ge(dve_mv, s.count(1))
                    dve.wait_ge(act_rstd, s.div(G))
                    for t in range(G):
                        row = x1[:, m, h * G + t, :]
                        v.tensor_scalar(row, row, y_mv[:, g, t, 0:1], rstd[:, g, t:t + 1],
                                        ALU.subtract, ALU.mult).then_inc(dve_x1, 1)
                if s.mod(T) == 2 and s.live(T):
                    dve.wait_ge(pe_mean, s.div(T))
                    v.tensor_scalar(meanT[:], ps_s[:, 0:C], 1.0 / NR, None, ALU.mult).then_inc(dve_meanT, 1)
                if s.mod(T) == 3 and s.live(T):
                    m = s.mod(2 * T, T) // T
                    n0 = s.div(T) * 5 - 5

                    def step(ins, k):
                        ins.then_inc(dve_routing, 1)
                        dve.wait_ge(dve_routing, n0 + k)

                    dve.wait_ge(pe_score, s.div(T))
                    step(v.tensor_tensor(sc[:], ps_s[0:1, 8:8 + E], rb[:], ALU.add), 1)
                    step(v.reduce_max(sc_max[:], sc[:], AX_X), 2)
                    step(v.tensor_scalar(sc[:], sc[:], sc_max[0:1, 0:1], float(E), ALU.is_lt, ALU.mult), 3)
                    step(v.tensor_tensor(sc[:], sc[:], iota_f[:], ALU.add), 4)
                    step(v.tensor_reduce(sc_idx[:], sc[:], AX_X, ALU.min), 5)
                    v.tensor_copy(sc_int[0:1, m:m + 1], sc_idx[:])
                    hot_at = hot_row[:].rearrange("o b e -> o (b e)")[:, bass.ds(s.div(T) * E - E, E)]
                    v.tensor_scalar(hot_at, iota_f[:], sc_idx[0:1, 0:1], None, ALU.is_equal).then_inc(dve_route, 1)

            run_slots(dve, body)

            done = [0]

            def then(ins):
                done[0] += 1
                ins.then_inc(dve_bn, 1)
                dve.wait_ge(dve_bn, done[0])

            dve.wait_ge(pe_hot, 1)
            then(v.tensor_copy(hot[:], ps_s[:, 64:64 + NB * E].rearrange("p (b e) -> p b e", b=NB)))
            dve.wait_ge(dve_omv, NB)
            mean = o_mv[:, :, :, 0]
            then(v.tensor_tensor(bn_a[:, 0:NB * C].rearrange("p (b c) -> p b c", b=NB), mean, mean, ALU.mult))
            then(v.tensor_tensor(o_mv[:, :, :, 1], o_mv[:, :, :, 1],
                                 bn_a[:, 0:NB * C].rearrange("p (b c) -> p b c", b=NB), ALU.add))
            for e in range(E):
                prod = bn_a[:, e * NB * C * 2:(e + 1) * NB * C * 2].rearrange("p (k b) -> p k b", b=NB)
                last = v.tensor_tensor(prod, o_mv[:].rearrange("p b c s -> p (c s) b"),
                                       hot[:, :, e].rearrange("p (o b) -> p o b", o=1).broadcast_to([P, 2 * C, NB]),
                                       ALU.mult)
            then(last)
            v.tensor_reduce(e_cnt[:], hot[:].rearrange("p b e -> p e b"), AX_X, ALU.add)
            then(v.tensor_reduce(e_sum[:].rearrange("p e k -> p (e k)"), bn_a.rearrange("p (k b) -> p k b", b=NB),
                                 AX_X, ALU.add))
            then(v.tensor_scalar(e_cnt[:], e_cnt[:], 1.0 / NR, None, ALU.max))
            then(v.reciprocal(e_cnt[:], e_cnt[:]))
            for e in range(E):
                last = v.tensor_scalar(e_sum[:, e, :], e_sum[:, e, :], e_cnt[:, e:e + 1], None, ALU.mult)
            then(last)
            e_mean = e_sum[:].rearrange("p e (c s) -> p e c s", s=2)[:, :, :, 0]
            e_msq = e_sum[:].rearrange("p e (c s) -> p e c s", s=2)[:, :, :, 1]
            then(v.tensor_tensor(e_bias[:], e_mean, e_mean, ALU.mult))
            then(v.tensor_tensor(e_sq[:], e_msq, e_bias[:], ALU.subtract))
            assert done[0] == BN_VAR
            dve.wait_ge(bn_landed, 16 * 2 * C)
            dve.wait_ge(act_bn, 2)
            then(v.tensor_tensor(e_scale[:], e_scale[:], gamT[:], ALU.mult))
            then(v.tensor_tensor(e_bias[:], e_mean, e_scale[:], ALU.mult))
            then(v.tensor_tensor(e_bias[:], betT[:], e_bias[:], ALU.subtract))
            for e_val, b_val in ((e_scale, b_scale), (e_bias, b_bias)):
                for c in range(C):
                    last = v.tensor_tensor(bn_a[:, c * NB * E:(c + 1) * NB * E].rearrange("p (b e) -> p b e", b=NB),
                                           hot[:], e_val[:, :, c].rearrange("p (o e) -> p o e", o=1)
                                           .broadcast_to([P, NB, E]), ALU.mult)
                then(last)
                then(v.tensor_reduce(b_val[:].rearrange("p b c -> p c b"),
                                     bn_a[:, 0:C * NB * E].rearrange("p (c b e) -> p c b e", c=C, b=NB),
                                     AX_X, ALU.add))
            assert done[0] == BN_DONE

            def rows(q, i):
                dve.wait_ge(x1_back[i], q * 16 + 16)
                for g in range(2):
                    groups = q * 8 + (i * 2 + g)
                    for t in range(G):
                        n = q * (4 * T) + (i * T + g * G + t)
                        row = y_buf[i][:, g * G + t, :]
                        dve.wait_ge(pe_back, n + 1)
                        v.tensor_tensor(row, ps_y[t % 4], row, ALU.add).then_inc(dve_y2, 1)
                        dve.wait_ge(dve_y2, n + 1)
                        v.bn_stats(y_stat[:, t % 2, :], row).then_inc(dve_stat2, 1)
                        dve.wait_ge(dve_stat2, n + 1)
                        v.memset(pad[:], 0.0)
                        v.bn_aggr(y_mv[:, g, t, :], y_stat[:, t % 2, :]).then_inc(dve_mv2, 1)
                    dve.wait_ge(dve_mv2, q * (4 * T) + (i * T + (g + 1) * G))
                    dve.wait_ge(act_rstd2, groups + 1)
                    wait(dve, act_out, q * (4 * T) + (i * T + (g - 1) * G))
                    v.scalar_tensor_tensor(out=nmr[:, g, :], in0=y_mv[:, g, :, 0], scalar=-1.0, in1=rstd[:, g, :],
                                           op0=ALU.mult, op1=ALU.mult).then_inc(dve_nmr2, 1)

            run_batches(dve, rows)

        @block.tensor
        def _(pe):
            te = nc.tensor
            pe.wait_ge(pool_const, 2)
            pe.wait_ge(w0_landed, 16)
            for c in range(C):
                if c >= 2:
                    pe.wait_ge(dve_w0, 2 + c - 1)
                for n in range(NK):
                    last = te.transpose(ps_adjT[:, c % 2, n * P:(n + 1) * P],
                                        wgt[:, 1, n, c * P:(c + 1) * P], ident[:])
                last.then_inc(pe_w0, 1)
            pe.wait_ge(dve_w0, 2 + C)
            pe.wait_ge(dve_const, 4)

            def body(s):
                if s.live():
                    a, m = s.mod(2), s.mod(2)
                    pe.wait_ge(adj_landed[a], s.div(2) * 16 + 16)
                    for h in range(2):
                        wait(pe, act_adjT, s.count(2, plus=h - 1))
                        for c in range(4):
                            j = 4 * h + c
                            last = te.transpose(ps_adjT[:, h, c * P:(c + 1) * P], adj_in[:, a, j * P:(j + 1) * P], ident[:])
                        last.then_inc(pe_adjT, 1)
                    pe.wait_ge(x_landed[s.mod(4)], s.div(4) * 16 + 16)
                    wait(pe, act_xT, s.count(1))
                    for c in range(C):
                        last = te.transpose(ps_xT[:, c * P:(c + 1) * P], x_in[:, s.mod(4), c * P:(c + 1) * P], ident[:])
                    last.then_inc(pe_xT, 1)
                if s.live(B_LAG):
                    b, half, k = s.mod(2 * T, B_LAG) // T, s.mod(T, B_LAG) // 4, s.mod(4, B_LAG)
                    if s.mod(T, B_LAG) == 0:
                        pe.wait_ge(dve_x1, s.count(1, plus=T, lag=B_LAG))
                        pe.wait_ge(act_adjT, s.count(2, plus=2 * T, lag=B_LAG))
                        wait(pe, dve_route, s.div(T, B_LAG))
                        for c in range(C):
                            for t in range(T):
                                last = te.matmul(ps_s[:, c:c + 1], x1[:, b, t, c * P:(c + 1) * P], ones[:, 0:1],
                                                 start=(t == 0), stop=(t == T - 1))
                        last.then_inc(pe_mean, 1)
                    wait(pe, act_z, s.count(1, plus=-1, lag=B_LAG))
                    for t in range(T):
                        last = te.matmul(ps_z[:, s.mod(2, B_LAG), :], x1[:, b, t, k * P:(k + 1) * P],
                                         adjT[:, b, t, half * HALF:(half + 1) * HALF], start=(t == 0), stop=(t == T - 1))
                    last.then_inc(pe_z, 1)
                if s.live(C_LAG):
                    b, half, k = s.mod(2 * T, C_LAG) // T, s.mod(T, C_LAG) // 4, s.mod(4, C_LAG)
                    if s.mod(T, C_LAG) == 0:
                        pe.wait_ge(w_landed[b], s.div(2 * T, C_LAG) * 16 + 16)
                    if k == 0:
                        pe.wait_ge(act_z, s.count(1, plus=4, lag=C_LAG))
                    wait(pe, act_o, s.count(1, lag=C_LAG))
                    for c in range(C):
                        last = te.matmul(ps_o[:], w_sel[:, b, c, k * P:(k + 1) * P], zT[:, half, c, :],
                                         start=(c == 0), stop=(c == C - 1))
                    last.then_inc(pe_o, 1)
                if s.live():
                    pe.wait_ge(act_xT, s.count(1, plus=1))
                    wait(pe, dve_y, s.count(1))
                    for c in range(C):
                        last = te.matmul(ps_h[:], xT[:, s.mod(2), c, :], w0T[:, c, :], start=(c == 0), stop=(c == C - 1))
                    last.then_inc(pe_h, 1)
                if s.mod(T) == 2 and s.live(T):
                    pe.wait_ge(dve_meanT, s.div(T))
                    for c in range(C):
                        last = te.matmul(ps_s[0:1, 8:8 + E], meanT[:, c:c + 1], rw[:, c, :],
                                         start=(c == 0), stop=(c == C - 1))
                    last.then_inc(pe_score, 1)

            run_slots(pe, body)

            pe.wait_ge(dve_route, NB)
            te.matmul(ps_s[:, 64:64 + NB * E], ones[0:1, :], hot_row[:].rearrange("o b e -> o (b e)"),
                      start=True, stop=True).then_inc(pe_hot, 1)

            def rows(q, i):
                pe.wait_ge(act_relu, q * (4 * C) + (i + 1) * C)
                for t in range(T):
                    wait(pe, dve_y2, q * (4 * T) + (i * T + t - 3))
                    for c in range(C):
                        last = te.transpose(ps_y[t % 4][:, c * P:(c + 1) * P], o_buf[i][:, c, t * P:(t + 1) * P], ident[:])
                    last.then_inc(pe_back, 1)

            run_batches(pe, rows)


_INS = ['x', 'adj', 'L0_gnn_mean_relation', 'L0_gnn_precision_relation', 'L0_gnn_W', 'L1_gnn_router_w',
        'L1_gnn_router_b', 'L1_gnn_expert_w', 'L1_gnn_bn_gamma', 'L1_gnn_bn_beta']


def kernel(**inputs):
    import numpy as _np
    import concourse.bacc as _bacc
    from concourse import mybir as _mybir
    from concourse.bass_utils import run_bass_kernel_spmd as _run

    nc = _bacc.Bacc("TRN2", target_bir_lowering=False, num_devices=1)
    arrays, args = {}, []
    for name in _INS:
        a = _np.ascontiguousarray(inputs[name])
        arrays[f"in_{name}_dram"] = a
        args.append(nc.dram_tensor(f"in_{name}_dram", a.shape, _mybir.dt.from_np(a.dtype), kind="ExternalInput").ap())
    nb, rows, width = inputs['x'].shape
    x1_spill = nc.dram_tensor("x1_spill", (nb, rows, width), F32, kind="Internal").ap()
    out_spill = nc.dram_tensor("out_spill", (nb, width, rows), F32, kind="Internal").ap()
    out = nc.dram_tensor("out_0_dram", (nb, rows, width), F32, kind="ExternalOutput").ap()
    gnn_program(nc, *args, x1_spill, out_spill, out)
    r = _run(nc, [arrays], core_ids=[0])
    return r.results[0]["out_0_dram"]
```

```python
from contextlib import ExitStack

import concourse.bass as bass
from concourse import mybir

ALU = mybir.AluOpType
ACT = mybir.ActivationFunctionType
F32 = mybir.dt.float32
F16 = mybir.dt.float16
I32 = mybir.dt.int32
AX_X = mybir.AxisListType.X

P = 128
LN_EPS = 1e-5
BN_EPS = 1e-5
SUM_SCALE = 2.0 ** 60
X_SCALE = 2.0 ** 4
W0_SCALE = 2.0 ** 8
ADJ_SCALE = 2.0 ** 10
X1_SCALE = 2.0 ** 8
SPAN = 16
B_LAG = 10
C_LAG = 14


class Slot:

    def __init__(self, p, r, total):
        self.p, self.r, self.total = p, r, total
        self.fixed = isinstance(p, int)

    def live(self, lag=0):
        return not self.fixed or 0 <= SPAN * self.p + self.r - lag < self.total

    def mod(self, m, lag=0):
        return (self.r - lag) % m

    def div(self, m, lag=0):
        return self.p * (SPAN // m) + (self.r - lag) // m

    def count(self, per=1, plus=0, lag=0):
        return self.p * (SPAN * per) + (per * (self.r - lag) + plus)


def wait(eng, sem, value):
    if isinstance(value, int) and value <= 0:
        return
    eng.wait_ge(sem, value)


def held(eng, value):
    return value if isinstance(value, int) else eng.to_reg(value)


def gnn_program(nc, x, adj, mean_rel, prec_rel, w0, router_w, router_b, expert_w, gamma, beta, x1_spill,
                out_spill, out):
    NB, NR, D = x.shape
    NK = mean_rel.shape[0]
    E = expert_w.shape[0]
    T = NR // P
    C = D // P
    G = 4
    HALF = NR // 2
    TILES = NB * T
    KW = D // NK
    assert T == 8 and C == 4 and NK == 4 and HALF == 512 and KW == P and TILES % SPAN == 0

    with ExitStack() as ctx:
        def sb(name, shape, dt=F32):
            return ctx.enter_context(nc.sbuf_tensor(name, shape, dt))

        def sem(name):
            return ctx.enter_context(nc.semaphore(name))

        def sems(name, n):
            return [sem(f"{name}{i}") for i in range(n)]

        adj_in = sb("adj_in", [P, 2, NR])
        x_in = sb("x_in", [P, T, D])
        adjT = sb("adjT", [P, 2, 2, T, NR], F16)
        x1p = sb("x1p", [P, 2, 2, T, D], F16)
        w_sel = sb("w_sel", [P, C, D])
        w0T = sb("w0T", [P, 2, C, D], F16)
        xT = sb("xT", [P, 2, 2, C, P], F16)
        wgt = sb("wgt", [P, 2, NK, NR])
        tot = sb("tot", [P, 2, NR])
        zT = sb("zT", [P, 2, C, HALF])
        o_stage = sb("o_stage", [P, 2, HALF])
        ident = sb("ident", [P, P])
        ones = sb("ones", [1, P])
        ones_h = sb("ones_h", [P, 2], F16)
        neg_mu = sb("neg_mu", [P, NK])
        neg_alpha = sb("neg_alpha", [P, NK])
        eps_x1 = sb("eps_x1", [P, 1])
        eps_bn = sb("eps_bn", [P, 1])
        eps_out = sb("eps_out", [P, 1])
        wsum = sb("wsum", [P, 2, NK])
        y_stat = sb("y_stat", [P, 2, 6])
        y_mv = sb("y_mv", [P, 2, G, 2])
        ln_var = sb("ln_var", [P, G])
        rstd = sb("rstd", [P, 2, G])
        nmr = sb("nmr", [P, 2, G])
        o_stat = sb("o_stat", [P, 2, C, 2, 6])
        o_agg = sb("o_agg", [P, C, 2])
        pad = sb("pad", [P, 1])
        o_mv = sb("o_mv", [P, NB, C, 2])
        rw = sb("rw", [P, C, E])
        rb = sb("rb", [1, E])
        iota_f = sb("iota_f", [1, E])
        iota_i = sb("iota_i", [1, E], I32)
        meanT = sb("meanT", [P, C])
        sc = sb("sc", [1, E])
        sc_max = sb("sc_max", [1, 1])
        sc_idx = sb("sc_idx", [1, 1])
        sc_int = sb("sc_int", [1, 2], I32)
        hot_row = sb("hot_row", [1, NB, E])
        hot = sb("hot", [P, NB, E])
        gamT = sb("gamT", [P, E, C])
        betT = sb("betT", [P, E, C])
        e_sum = sb("e_sum", [P, E, 2 * C])
        e_cnt = sb("e_cnt", [P, E])
        e_sq = sb("e_sq", [P, E, C])
        e_lnv = sb("e_lnv", [P, E, C])
        e_scale = sb("e_scale", [P, E, C])
        e_bias = sb("e_bias", [P, E, C])
        b_scale = sb("b_scale", [P, NB, C])
        b_bias = sb("b_bias", [P, NB, C])

        ps_adjT = ctx.enter_context(nc.psum_tensor("ps_adjT", [P, 2, 512], F32))
        ps_xT = ctx.enter_context(nc.psum_tensor("ps_xT", [P, 512], F32))
        ps_h = ctx.enter_context(nc.psum_tensor("ps_h", [P, 512], F32))
        ps_z = ctx.enter_context(nc.psum_tensor("ps_z", [P, 2, 512], F32))
        ps_o = ctx.enter_context(nc.psum_tensor("ps_o", [P, 512], F32))
        ps_s = ctx.enter_context(nc.psum_tensor("ps_s", [P, 512], F32))

        adj_landed = sems("adj_landed", 2)
        x_landed = sems("x_landed", T)
        w_landed = sem("w_landed")
        o_stored = sems("o_stored", 2)
        x1_stored = sems("x1_stored", 2)
        const_landed = sem("const_landed")
        w0_landed = sem("w0_landed")
        bn_landed = sem("bn_landed")
        pe_adjT, pe_xT, pe_h, pe_z, pe_o = (sem(f"pe_{k}") for k in ("adjT", "xT", "h", "z", "o"))
        pe_mean, pe_score, pe_w0, pe_hot, pe_back = (sem(f"pe_{k}") for k in ("mean", "score", "w0", "hot", "back"))
        act_sq, act_w, act_adjT, act_xT = (sem(f"act_{k}") for k in ("sq", "w", "adjT", "xT"))
        act_ln, act_rec, act_z, act_o = (sem(f"act_{k}") for k in ("ln", "rec", "z", "o"))
        act_lnv, act_rstd, act_bn, act_relu = (sem(f"act_{k}") for k in ("lnv", "rstd", "bn", "relu"))
        act_lnv2, act_rstd2, act_out = (sem(f"act_{k}") for k in ("lnv2", "rstd2", "out"))
        dve_tot, dve_ws, dve_y, dve_stat, dve_mv = (sem(f"dve_{k}") for k in ("tot", "ws", "y", "stat", "mv"))
        dve_x1, dve_ostat, dve_omv, dve_meanT = (sem(f"dve_{k}") for k in ("x1", "ostat", "omv", "meanT"))
        dve_routing, dve_oagg = sem("dve_routing"), sem("dve_oagg")
        dve_route, dve_const, dve_w0, dve_bn = (sem(f"dve_{k}") for k in ("route", "const", "w0", "bn"))
        dve_y2, dve_stat2, dve_mv2, dve_nmr2 = (sem(f"dve_{k}") for k in ("y2", "stat2", "mv2", "nmr2"))
        dve_xT, dve_adjT = sem("dve_xT"), sem("dve_adjT")
        pool_const, pool_hi, pool_x1 = sem("pool_const"), sem("pool_hi"), sem("pool_x1")
        o_back, x1_back, y_stored = sems("o_back", 4), sems("x1_back", 4), sems("y_stored", 4)

        wgt_flat = wgt[:].rearrange("p a k n -> p (a k n)")
        adjT_flat = adjT[:].rearrange("p a h t n -> p (a h t n)").bitcast(F32)
        x1p_flat = x1p[:].rearrange("p a h t n -> p (a h t n)").bitcast(F32)
        bn_a = tot[:, 0, 0:2 * NB * C * E]
        BUF = T * D
        areas = [wgt_flat[:, 0:BUF], x_in[:].rearrange("p t n -> p (t n)"),
                 adjT_flat[:, 0:BUF], adjT_flat[:, BUF:2 * BUF],
                 wgt_flat[:, BUF:2 * BUF], x1p_flat[:, 0:BUF],
                 adjT_flat[:, 2 * BUF:3 * BUF], adjT_flat[:, 3 * BUF:4 * BUF]]
        o_buf = [areas[2 * i].rearrange("p (c n) -> p c n", c=C) for i in range(4)]
        y_buf = [areas[2 * i + 1].rearrange("p (t n) -> p t n", t=T) for i in range(4)]
        ps_y = [ps_adjT[:, 0, :], ps_adjT[:, 1, :], ps_xT[:], ps_h[:]]

        PAIRS = TILES // SPAN
        LAST = TILES + C_LAG + 1

        def run_slots(eng, body):
            for r in range(SPAN):
                body(Slot(0, r, TILES))
            with eng.Fori(1, PAIRS) as p:
                for r in range(SPAN):
                    body(Slot(p, r, TILES))
            for n in range(TILES, LAST):
                body(Slot(PAIRS, n - TILES, TILES))

        def run_batches(eng, body):
            for i in range(4):
                body(0, i)
            with eng.Fori(1, NB // 4) as q:
                for i in range(4):
                    body(q, i)

        def batch_of(q, i):
            return NB - 1 if isinstance(q, int) and q == 0 and i == 0 else q * 4 + (i - 1)

        def kept(unit):
            return unit.fixed and SPAN * unit.p + unit.r - (C_LAG + 1) >= TILES - T

        def out_unit(s):
            half, k = s.mod(T, C_LAG + 1) // 4, s.mod(4, C_LAG + 1)
            return o_buf[0][:, k, half * HALF:(half + 1) * HALF] if kept(s) else o_stage[:, k % 2, :]

        BN_VAR, BN_DONE = 10, 18

        block = ctx.enter_context(nc.Block())

        @block.sync
        def _(sp):
            sp.dma_start(neg_mu[:], mean_rel.rearrange("(o k) -> o k", o=1).broadcast_to([P, NK])).then_inc(const_landed, 16)
            sp.dma_start(neg_alpha[:], prec_rel.rearrange("(o k) -> o k", o=1).broadcast_to([P, NK])).then_inc(const_landed, 16)

            def load_adj(s, ahead):
                squared = held(sp, s.count(4, plus=4 * (ahead - 1)))
                transposed = held(sp, s.count(2, plus=2 * (ahead - 1)))
                wait(sp, act_sq, squared)
                wait(sp, pe_adjT, transposed)
                k = s.mod(2, -ahead)
                src = adj.rearrange("b (t p) n -> (b t) p n", p=P)[s.count(1, plus=ahead)]
                sp.dma_start(adj_in[:, k, :], src).then_inc(adj_landed[k], 16)

            def load_x(s, ahead):
                if s.mod(G, T - ahead) == 0 and s.live(T - ahead):
                    split = held(sp, s.count(1, plus=G, lag=T - ahead))
                    stored = held(sp, s.div(T, T - ahead) * 16 + 16)
                    wait(sp, pool_x1, split)
                    wait(sp, x1_stored[s.mod(T, T - ahead) // G], stored)
                k = s.mod(T, -ahead)
                src = x.rearrange("b (t p) n -> (b t) p n", p=P)[s.count(1, plus=ahead)]
                sp.dma_start(x_in[:, k, :], src).then_inc(x_landed[k], 16)

            for k in range(2):
                sp.dma_start(adj_in[:, k, :], adj[0, k * P:(k + 1) * P, :]).then_inc(adj_landed[k], 16)
                sp.dma_start(x_in[:, k, :], x[0, k * P:(k + 1) * P, :]).then_inc(x_landed[k], 16)
                if k == 0:
                    sp.dma_start(wgt[:, 1, :, 0:D], w0.rearrange("n o d -> o n d")).then_inc(w0_landed, 16)
            sp.dma_start(rw[:], router_w.rearrange("(c p) e -> p c e", p=P)).then_inc(const_landed, 16)
            sp.dma_start(rb[:], router_b.rearrange("(o e) -> o e", o=1)).then_inc(const_landed, 16)

            def body(s):
                fetch = s.mod(T, C_LAG) == 0 and s.live(C_LAG)
                if fetch:
                    routed = held(sp, s.div(T, C_LAG) + 1)
                    used = held(sp, s.count(1, lag=C_LAG))
                    wait(sp, dve_route, routed)
                    wait(sp, pe_o, used)
                if s.live(-2):
                    load_x(s, 2)
                if fetch:
                    m = s.mod(2 * T, C_LAG) // T
                    e = sp.value_load(sc_int[0:1, m:m + 1], min_val=0, max_val=E - 1)
                    sp.dma_start(w_sel[:], expert_w.rearrange("e (c p) k -> e p c k", p=P)[e]).then_inc(w_landed, 16)
                if s.live(-2):
                    load_adj(s, 2)

            for r in range(SPAN):
                body(Slot(0, r, TILES))
            with sp.Fori(1, PAIRS - 1) as p:
                for r in range(SPAN):
                    body(Slot(p, r, TILES))
            for n in range(TILES - SPAN, LAST):
                body(Slot(n // SPAN, n % SPAN, TILES))

            def back(q, i):
                b = batch_of(q, i)
                first = isinstance(q, int) and q == 0
                if first and i == 0:
                    return
                if first:
                    sp.wait_ge(pe_z, TILES if i == 3 else TILES - T)
                    if i == 2:
                        sp.wait_ge(dve_ws, TILES)
                else:
                    sp.wait_ge(y_stored[i], q * 32)
                    if i > 0:
                        sp.wait_ge(o_back[i], q * 16)
                        sp.wait_ge(x1_back[i], q * 16)
                for k in range(2):
                    sp.wait_ge(o_stored[k], q * 256 + i * 64)
                    sp.wait_ge(x1_stored[k], q * 64 + i * 16)
                sp.dma_start(o_buf[i], out_spill.rearrange("b (c p) n -> b p c n", p=P)[b]).then_inc(o_back[i], 16)
                sp.dma_start(y_buf[i], x1_spill.rearrange("b (t p) n -> b p t n", p=P)[b]).then_inc(x1_back[i], 16)

            for i in range(4):
                back(0, i)
            with sp.Fori(1, NB // 4) as q:
                for i in range(4):
                    back(q, i)

        @block.gpsimd
        def _(pool):
            nc.gpsimd.memset(ident[:], 0.0).then_inc(pool_const, 1)
            pool.wait_ge(pool_const, 1)
            nc.gpsimd.affine_select(out=ident[:], in_=ident[:], compare_op=ALU.not_equal, fill=1.0, base=0,
                                    pattern=[[-1, P]], channel_multiplier=1).then_inc(pool_const, 1)
            nc.gpsimd.iota(iota_i[:], pattern=[[1, E]], base=0, channel_multiplier=0).then_inc(pool_const, 1)
            with nc.allow_non_contiguous_dma("two small transposed tables"):
                for k in range(C):
                    pool.dma_start(gamT[:, :, k], gamma[:, k * P:(k + 1) * P].rearrange("e p -> p e")).then_inc(bn_landed, 16)
                    pool.dma_start(betT[:, :, k], beta[:, k * P:(k + 1) * P].rearrange("e p -> p e")).then_inc(bn_landed, 16)

            def body(s):
                if s.mod(G) == 1 and s.live(G + 1):
                    pool.wait_ge(dve_x1, s.count(1, lag=1))
                    g = s.mod(SPAN, G + 1) // G
                    h, m = g % 2, g // 2
                    if h == 0:
                        wait(pool, pe_z, s.count(1, plus=-T, lag=G + 1))
                    dst = x1_spill.rearrange("b (g t p) n -> (b g) p t n", g=2, p=P)[s.div(G, G + 1)]
                    pool.dma_start(dst, x_in[:, h * G:(h + 1) * G, :]).then_inc(x1_stored[h], 16)
                    for t in range(h * G, (h + 1) * G):
                        nc.gpsimd.tensor_scalar(x1p[:, m, 0, t, :], x_in[:, t, :], 1.0, 1.0, ALU.mult,
                                                ALU.mult).then_inc(pool_hi, 1)
                        pool.wait_ge(pool_hi, s.count(1, plus=t - h * G + 1, lag=G + 1))
                        nc.gpsimd.tensor_tensor(x1p[:, m, 1, t, :], x_in[:, t, :], x1p[:, m, 0, t, :],
                                                ALU.subtract).then_inc(pool_x1, 1)
                if s.live(C_LAG + 1) and not kept(s):
                    pool.wait_ge(act_o, s.count(1, plus=1, lag=C_LAG + 1))
                    k = s.mod(4, C_LAG + 1)
                    half = s.mod(T, C_LAG + 1) // 4
                    dst = out_spill.rearrange("b (c p) n -> b c p n", p=P)[
                        s.div(T, C_LAG + 1), k, :, half * HALF:(half + 1) * HALF]
                    pool.dma_start(dst, o_stage[:, k % 2, :]).then_inc(o_stored[k % 2], 16)

            run_slots(pool, body)

            def out_rows(q, i):
                for g in range(2):
                    pool.wait_ge(act_out, q * (4 * T) + i * T + (g + 1) * G)
                    dst = out.rearrange("b (g t p) n -> b g p t n", g=2, p=P)[batch_of(q, i), g]
                    pool.dma_start(dst, y_buf[i][:, g * G:(g + 1) * G, :]).then_inc(y_stored[i], 16)

            run_batches(pool, out_rows)
            for i in range(4):
                pool.wait_ge(y_stored[i], NB // 4 * 32)

        @block.scalar
        def _(act):
            nc.scalar.preload_act_table_set("natural_log_exp_and_others")
            act.wait_ge(dve_const, 2)

            def body(s):
                if s.live(C_LAG + 1):
                    k = s.mod(4, C_LAG + 1)
                    act.wait_ge(pe_o, s.count(1, plus=1, lag=C_LAG + 1))
                    if kept(s):
                        act.wait_ge(dve_ws, TILES)
                    else:
                        wait(act, o_stored[k % 2], s.div(2, C_LAG + 1) * 16)
                        wait(act, dve_ostat, s.count(1, lag=C_LAG + 1))
                    nc.scalar.activation(out_unit(s), ps_o[:], ACT.Copy).then_inc(act_o, 1)
                if s.live():
                    a, m = s.mod(2), s.mod(2)
                    act.wait_ge(adj_landed[a], s.div(2) * 16 + 16)
                    wait(act, dve_ws, s.count(1, plus=-1))
                    if s.fixed and s.p == 0 and s.r == 1:
                        act.wait_ge(pe_w0, C)
                    def square(k):
                        nc.scalar.activation(wgt[:, m, k, :], adj_in[:, a, :], ACT.Square,
                                             bias=neg_mu[:, k:k + 1]).then_inc(act_sq, 1)

                    def weigh(k):
                        act.wait_ge(act_sq, s.count(4, plus=k + 1))
                        nc.scalar.activation(wgt[:, m, k, :], wgt[:, m, k, :], ACT.Exp,
                                             scale=neg_alpha[:, k:k + 1]).then_inc(act_w, 1)

                    square(0)
                    square(1)
                    act.wait_ge(pe_xT, s.count(1, plus=1))
                    wait(act, pe_h, s.count(1, plus=-1))
                    nc.scalar.activation(xT[:, m, 0, :, :].rearrange("p c n -> p (c n)"), ps_xT[:],
                                         ACT.Copy, scale=X_SCALE).then_inc(act_xT, 1)
                    weigh(0)
                    for k in range(1, NK - 1):
                        square(k + 1)
                        weigh(k)
                    weigh(NK - 1)
                    b, t = s.mod(2 * T) // T, s.mod(T)
                    if t % 4 == 0:
                        wait(act, pe_z, s.count(1, plus=-12))
                    for h in range(2):
                        act.wait_ge(pe_adjT, s.count(2, plus=h + 1))
                        nc.scalar.activation(adjT[:, b, 0, 4 * h:4 * h + 4, t * P:(t + 1) * P],
                                             ps_adjT[:, h, :].rearrange("p (c n) -> p c n", c=4),
                                             ACT.Copy, scale=ADJ_SCALE).then_inc(act_adjT, 1)
                if s.live(B_LAG):
                    u, half, k = s.mod(2, B_LAG), s.mod(T, B_LAG) // 4, s.mod(4, B_LAG)
                    act.wait_ge(pe_z, s.count(1, plus=1, lag=B_LAG))
                    if k == 0:
                        wait(act, pe_o, s.count(1, plus=-4, lag=B_LAG))
                    nc.scalar.activation(zT[:, half, k, :], ps_z[:, u, :], ACT.Copy,
                                         scale=1.0 / (ADJ_SCALE * X1_SCALE)).then_inc(act_z, 1)
                if s.mod(G) == 0 and s.live(G):
                    g = s.mod(2 * G, G) // G
                    act.wait_ge(dve_mv, s.count(1))
                    nc.scalar.activation(ln_var[:], y_mv[:, g, :, 1], ACT.Ln, bias=eps_x1[:, 0:1],
                                         scale=X1_SCALE ** -2).then_inc(act_lnv, 1)
                    act.wait_ge(act_lnv, s.div(G))
                    nc.scalar.activation(rstd[:, g, :], ln_var[:], ACT.Exp, scale=-0.5).then_inc(act_rstd, 1)
                if s.live():
                    act.wait_ge(dve_tot, s.count(3, plus=3))
                    nc.scalar.activation(tot[:, m, :], tot[:, m, :], ACT.Ln, scale=SUM_SCALE).then_inc(act_ln, 1)
                    act.wait_ge(act_ln, s.count(1, plus=1))
                    nc.scalar.activation(tot[:, m, :], tot[:, m, :], ACT.Exp, scale=-1.0).then_inc(act_rec, 1)

            run_slots(act, body)

            act.wait_ge(dve_bn, BN_VAR)
            nc.scalar.activation(e_lnv[:], e_sq[:], ACT.Ln, bias=eps_bn[:, 0:1]).then_inc(act_bn, 1)
            act.wait_ge(act_bn, 1)
            nc.scalar.activation(e_scale[:], e_lnv[:], ACT.Exp, scale=-0.5).then_inc(act_bn, 1)
            act.wait_ge(dve_bn, BN_DONE)

            def rows(q, i):
                if i == 0:
                    wait(act, o_back[i], q * 16)
                    act.wait_ge(act_o, TILES)
                else:
                    act.wait_ge(o_back[i], q * 16 + 16)
                for k in range(C):
                    nc.scalar.activation(o_buf[i][:, k, :], o_buf[i][:, k, :], ACT.Relu,
                                         bias=q_bias(q, i, k), scale=q_scale(q, i, k)).then_inc(act_relu, 1)
                for g in range(2):
                    done = q * (4 * T) + (i * T + g * G)
                    groups = q * 8 + (i * 2 + g)
                    act.wait_ge(dve_mv2, done + G)
                    nc.scalar.activation(ln_var[:], y_mv[:, g, :, 1], ACT.Ln, bias=eps_out[:, 0:1]).then_inc(act_lnv2, 1)
                    act.wait_ge(act_lnv2, groups + 1)
                    nc.scalar.activation(rstd[:, g, :], ln_var[:], ACT.Exp, scale=-0.5).then_inc(act_rstd2, 1)
                    act.wait_ge(act_rstd2, groups + 1)
                    act.wait_ge(dve_nmr2, groups + 1)
                    for t in range(G):
                        row = y_buf[i][:, g * G + t, :]
                        nc.scalar.activation(row, row, ACT.Identity, bias=nmr[:, g, t:t + 1],
                                             scale=rstd[:, g, t:t + 1]).then_inc(act_out, 1)

            def q_scale(q, i, k):
                return b_scale[:].rearrange("p b c -> p (b c)")[:, bass.ds(batch_of(q, i) * C + k, 1)]

            def q_bias(q, i, k):
                return b_bias[:].rearrange("p b c -> p (b c)")[:, bass.ds(batch_of(q, i) * C + k, 1)]

            run_batches(act, rows)


        @block.vector
        def _(dve):
            v = nc.vector
            v.memset(ones[:], 1.0)
            v.memset(ones_h[:], 1.0)
            v.memset(eps_x1[:], LN_EPS * X1_SCALE ** -2)
            v.memset(eps_bn[:], BN_EPS)
            v.memset(eps_out[:], LN_EPS * X1_SCALE ** 2)
            dve.wait_ge(const_landed, 64)
            v.tensor_tensor(neg_alpha[:], neg_alpha[:], neg_alpha[:], ALU.mult).then_inc(dve_w0, 1)
            dve.wait_ge(dve_w0, 1)
            v.tensor_scalar(neg_alpha[:], neg_alpha[:], 1e-14, -2.0, ALU.add, ALU.mult).then_inc(dve_w0, 1)
            dve.wait_ge(dve_w0, 2)
            v.reciprocal(neg_alpha[:], neg_alpha[:]).then_inc(dve_const, 1)
            v.tensor_scalar(neg_mu[:], neg_mu[:], -1.0, None, ALU.mult).then_inc(dve_const, 1)
            dve.wait_ge(pool_const, 3)
            v.tensor_copy(iota_f[:], iota_i[:]).then_inc(dve_const, 1)
            for c in range(C):
                dve.wait_ge(pe_w0, c + 1)
                v.tensor_scalar(w0T[:, 0, c, :], ps_adjT[:, c % 2, :], W0_SCALE, None, ALU.mult).then_inc(dve_w0, 1)
                dve.wait_ge(dve_w0, 2 * c + 3)
                v.scalar_tensor_tensor(out=w0T[:, 1, c, :], in0=ps_adjT[:, c % 2, :], scalar=W0_SCALE,
                                       in1=w0T[:, 0, c, :], op0=ALU.mult, op1=ALU.subtract).then_inc(dve_w0, 1)

            def body(s):
                if s.live():
                    dve.wait_ge(act_xT, s.count(1, plus=1))
                    v.scalar_tensor_tensor(out=xT[:, s.mod(2), 1, :, :].rearrange("p c n -> p (c n)"), in0=ps_xT[:],
                                           scalar=X_SCALE, in1=xT[:, s.mod(2), 0, :, :].rearrange("p c n -> p (c n)"),
                                           op0=ALU.mult, op1=ALU.subtract).then_inc(dve_xT, 1)
                if s.live():
                    m = s.mod(2)
                    wait(dve, dve_stat, s.count(1))
                    dve.wait_ge(act_w, s.count(4, plus=2))
                    v.tensor_tensor(tot[:, m, :], wgt[:, m, 0, :], wgt[:, m, 1, :], ALU.add).then_inc(dve_tot, 1)
                    for k in range(2, NK):
                        dve.wait_ge(act_w, s.count(4, plus=k + 1))
                        dve.wait_ge(dve_tot, s.count(3, plus=k - 1))
                        v.tensor_tensor(tot[:, m, :], tot[:, m, :], wgt[:, m, k, :], ALU.add).then_inc(dve_tot, 1)
                if s.live(1):
                    g, tg = s.mod(2 * G, 1) // G, s.mod(G, 1)
                    if not s.live():
                        dve.wait_ge(dve_stat, s.count(1))
                    v.bn_aggr(y_mv[:, g, tg, :], y_stat[:, s.mod(2, 1), :]).then_inc(dve_mv, 1)
                if s.live():
                    b, t = s.mod(2 * T) // T, s.mod(T)
                    for h in range(2):
                        dve.wait_ge(act_adjT, s.count(2, plus=h + 1))
                        v.scalar_tensor_tensor(out=adjT[:, b, 1, 4 * h:4 * h + 4, t * P:(t + 1) * P],
                                               in0=ps_adjT[:, h, :].rearrange("p (c n) -> p c n", c=4), scalar=ADJ_SCALE,
                                               in1=adjT[:, b, 0, 4 * h:4 * h + 4, t * P:(t + 1) * P],
                                               op0=ALU.mult, op1=ALU.subtract).then_inc(dve_adjT, 1)
                if s.live(C_LAG + 1):
                    half, k = s.mod(T, C_LAG + 1) // 4, s.mod(4, C_LAG + 1)
                    m = s.mod(2 * T, C_LAG + 1) // T
                    dve.wait_ge(act_o, s.count(1, plus=1, lag=C_LAG + 1))
                    v.bn_stats(o_stat[:, m, k, half, :], out_unit(s)).then_inc(dve_ostat, 1)
                    if half == 1 and k == 3:
                        dve.wait_ge(dve_ostat, s.count(1, plus=1, lag=C_LAG + 1))
                        v.memset(pad[:], 0.0)
                        for c in range(C):
                            last = v.bn_aggr(o_agg[:, c, :], o_stat[:, m, c, :, :].rearrange("p h s -> p (h s)"))
                        last.then_inc(dve_oagg, 1)
                        dve.wait_ge(dve_oagg, s.div(T, C_LAG + 1) + 1)
                        v.tensor_copy(o_mv[:].rearrange("p b c s -> p (b c s)")[
                            :, bass.ds(s.div(T, C_LAG + 1) * (2 * C), 2 * C)],
                            o_agg[:].rearrange("p c s -> p (c s)")).then_inc(dve_omv, 1)
                if s.mod(G) == 0 and s.live(G):
                    g, h = s.mod(2 * G, G) // G, s.mod(T, G) // G
                    dve.wait_ge(dve_mv, s.count(1))
                    dve.wait_ge(act_rstd, s.div(G))
                    for t in range(G):
                        row = x_in[:, h * G + t, :]
                        v.tensor_scalar(row, row, y_mv[:, g, t, 0:1], rstd[:, g, t:t + 1],
                                        ALU.subtract, ALU.mult).then_inc(dve_x1, 1)
                if s.mod(T) == 3 and s.live(T):
                    dve.wait_ge(pe_mean, s.div(T))
                    v.tensor_scalar(meanT[:], ps_s[:, 0:C], 1.0 / (NR * X1_SCALE), None, ALU.mult).then_inc(dve_meanT, 1)
                if s.live():
                    j, t = s.mod(2), s.mod(T)
                    dve.wait_ge(act_rec, s.count(1, plus=1))
                    for k in range(NK):
                        v_ws = v.scalar_tensor_tensor(out=wgt[:, j, k, :], in0=wgt[:, j, k, :], scalar=SUM_SCALE / (X_SCALE * W0_SCALE),
                                                      in1=tot[:, j, :], op0=ALU.mult, op1=ALU.mult,
                                                      accum_out=wsum[:, j, k:k + 1])
                    v_ws.then_inc(dve_ws, 1)
                    dve.wait_ge(dve_ws, s.count(1, plus=1))
                    dve.wait_ge(pe_h, s.count(1, plus=1))
                    dve.wait_ge(x_landed[t], s.div(T) * 16 + 16)
                    for k in range(NK):
                        f = slice(k * KW, (k + 1) * KW)
                        v_y = v.scalar_tensor_tensor(out=x_in[:, t, f], in0=ps_h[:, f], scalar=wsum[:, j, k:k + 1],
                                                     in1=x_in[:, t, f], op0=ALU.mult, op1=ALU.add)
                    v_y.then_inc(dve_y, 1)
                    dve.wait_ge(dve_y, s.count(1, plus=1))
                    v.bn_stats(y_stat[:, j, :], x_in[:, t, :]).then_inc(dve_stat, 1)
                if s.mod(T) == 4 and s.live(T):
                    m = s.mod(2 * T, T) // T
                    n0 = s.div(T) * 5 - 5

                    def step(ins, k):
                        ins.then_inc(dve_routing, 1)
                        dve.wait_ge(dve_routing, n0 + k)

                    dve.wait_ge(pe_score, s.div(T))
                    step(v.tensor_tensor(sc[:], ps_s[0:1, 8:8 + E], rb[:], ALU.add), 1)
                    step(v.reduce_max(sc_max[:], sc[:], AX_X), 2)
                    step(v.tensor_scalar(sc[:], sc[:], sc_max[0:1, 0:1], float(E), ALU.is_lt, ALU.mult), 3)
                    step(v.tensor_tensor(sc[:], sc[:], iota_f[:], ALU.add), 4)
                    step(v.tensor_reduce(sc_idx[:], sc[:], AX_X, ALU.min), 5)
                    v.tensor_copy(sc_int[0:1, m:m + 1], sc_idx[:])
                    hot_at = hot_row[:].rearrange("o b e -> o (b e)")[:, bass.ds(s.div(T) * E - E, E)]
                    v.tensor_scalar(hot_at, iota_f[:], sc_idx[0:1, 0:1], None, ALU.is_equal).then_inc(dve_route, 1)

            run_slots(dve, body)

            done = [0]

            def then(ins):
                done[0] += 1
                ins.then_inc(dve_bn, 1)
                dve.wait_ge(dve_bn, done[0])

            dve.wait_ge(pe_hot, 1)
            then(v.tensor_copy(hot[:], ps_s[:, 64:64 + NB * E].rearrange("p (b e) -> p b e", b=NB)))
            dve.wait_ge(dve_omv, NB)
            mean = o_mv[:, :, :, 0]
            then(v.tensor_tensor(bn_a[:, 0:NB * C].rearrange("p (b c) -> p b c", b=NB), mean, mean, ALU.mult))
            then(v.tensor_tensor(o_mv[:, :, :, 1], o_mv[:, :, :, 1],
                                 bn_a[:, 0:NB * C].rearrange("p (b c) -> p b c", b=NB), ALU.add))
            for e in range(E):
                prod = bn_a[:, e * NB * C * 2:(e + 1) * NB * C * 2].rearrange("p (k b) -> p k b", b=NB)
                last = v.tensor_tensor(prod, o_mv[:].rearrange("p b c s -> p (c s) b"),
                                       hot[:, :, e].rearrange("p (o b) -> p o b", o=1).broadcast_to([P, 2 * C, NB]),
                                       ALU.mult)
            then(last)
            v.tensor_reduce(e_cnt[:], hot[:].rearrange("p b e -> p e b"), AX_X, ALU.add)
            then(v.tensor_reduce(e_sum[:].rearrange("p e k -> p (e k)"), bn_a.rearrange("p (k b) -> p k b", b=NB),
                                 AX_X, ALU.add))
            then(v.tensor_scalar(e_cnt[:], e_cnt[:], 1.0 / NR, None, ALU.max))
            then(v.reciprocal(e_cnt[:], e_cnt[:]))
            for e in range(E):
                last = v.tensor_scalar(e_sum[:, e, :], e_sum[:, e, :], e_cnt[:, e:e + 1], None, ALU.mult)
            then(last)
            e_mean = e_sum[:].rearrange("p e (c s) -> p e c s", s=2)[:, :, :, 0]
            e_msq = e_sum[:].rearrange("p e (c s) -> p e c s", s=2)[:, :, :, 1]
            then(v.tensor_tensor(e_bias[:], e_mean, e_mean, ALU.mult))
            then(v.tensor_tensor(e_sq[:], e_msq, e_bias[:], ALU.subtract))
            assert done[0] == BN_VAR
            dve.wait_ge(bn_landed, 16 * 2 * C)
            dve.wait_ge(act_bn, 2)
            v.tensor_scalar(betT[:], betT[:], X1_SCALE, None, ALU.mult)
            then(v.tensor_tensor(e_scale[:], e_scale[:], gamT[:], ALU.mult))
            then(v.tensor_scalar(e_scale[:], e_scale[:], X1_SCALE, None, ALU.mult))
            then(v.tensor_tensor(e_bias[:], e_mean, e_scale[:], ALU.mult))
            then(v.tensor_tensor(e_bias[:], betT[:], e_bias[:], ALU.subtract))
            for e_val, b_val in ((e_scale, b_scale), (e_bias, b_bias)):
                for c in range(C):
                    last = v.tensor_tensor(bn_a[:, c * NB * E:(c + 1) * NB * E].rearrange("p (b e) -> p b e", b=NB),
                                           hot[:], e_val[:, :, c].rearrange("p (o e) -> p o e", o=1)
                                           .broadcast_to([P, NB, E]), ALU.mult)
                then(last)
                then(v.tensor_reduce(b_val[:].rearrange("p b c -> p c b"),
                                     bn_a[:, 0:C * NB * E].rearrange("p (c b e) -> p c b e", c=C, b=NB),
                                     AX_X, ALU.add))
            assert done[0] == BN_DONE

            def rows(q, i):
                if i == 0:
                    wait(dve, x1_back[i], q * 16)
                    dve.wait_ge(dve_x1, TILES)
                else:
                    dve.wait_ge(x1_back[i], q * 16 + 16)
                for g in range(2):
                    groups = q * 8 + (i * 2 + g)
                    for t in range(G):
                        n = q * (4 * T) + (i * T + g * G + t)
                        row = y_buf[i][:, g * G + t, :]
                        dve.wait_ge(pe_back, n + 1)
                        v.tensor_tensor(row, ps_y[t % 4], row, ALU.add).then_inc(dve_y2, 1)
                        dve.wait_ge(dve_y2, n + 1)
                        v.bn_stats(y_stat[:, t % 2, :], row).then_inc(dve_stat2, 1)
                        dve.wait_ge(dve_stat2, n + 1)
                        v.memset(pad[:], 0.0)
                        v.bn_aggr(y_mv[:, g, t, :], y_stat[:, t % 2, :]).then_inc(dve_mv2, 1)
                    dve.wait_ge(dve_mv2, q * (4 * T) + (i * T + (g + 1) * G))
                    dve.wait_ge(act_rstd2, groups + 1)
                    wait(dve, act_out, q * (4 * T) + (i * T + (g - 1) * G))
                    v.scalar_tensor_tensor(out=nmr[:, g, :], in0=y_mv[:, g, :, 0], scalar=-1.0, in1=rstd[:, g, :],
                                           op0=ALU.mult, op1=ALU.mult).then_inc(dve_nmr2, 1)

            run_batches(dve, rows)

        @block.tensor
        def _(pe):
            te = nc.tensor
            PARTS = ((0, 0), (0, 1), (1, 0))
            pe.wait_ge(pool_const, 2)
            pe.wait_ge(w0_landed, 16)
            for c in range(C):
                if c >= 2:
                    pe.wait_ge(dve_w0, 2 * c)
                for n in range(NK):
                    last = te.transpose(ps_adjT[:, c % 2, n * P:(n + 1) * P],
                                        wgt[:, 1, n, c * P:(c + 1) * P], ident[:])
                last.then_inc(pe_w0, 1)
            pe.wait_ge(dve_w0, 2 + 2 * C)
            pe.wait_ge(dve_const, 3)

            def body(s):
                if s.live():
                    a, m = s.mod(2), s.mod(2)
                    pe.wait_ge(adj_landed[a], s.div(2) * 16 + 16)
                    for h in range(2):
                        wait(pe, dve_adjT, s.count(2, plus=h - 1))
                        for c in range(4):
                            j = 4 * h + c
                            last = te.transpose(ps_adjT[:, h, c * P:(c + 1) * P], adj_in[:, a, j * P:(j + 1) * P], ident[:])
                        last.then_inc(pe_adjT, 1)
                    pe.wait_ge(x_landed[s.mod(T)], s.div(T) * 16 + 16)
                    wait(pe, dve_xT, s.count(1))
                    for c in range(C):
                        last = te.transpose(ps_xT[:, c * P:(c + 1) * P], x_in[:, s.mod(T), c * P:(c + 1) * P], ident[:])
                    last.then_inc(pe_xT, 1)
                if s.live(B_LAG):
                    b, half, k = s.mod(2 * T, B_LAG) // T, s.mod(T, B_LAG) // 4, s.mod(4, B_LAG)
                    if s.mod(T, B_LAG) == 0:
                        pe.wait_ge(pool_x1, s.count(1, plus=T, lag=B_LAG))
                        pe.wait_ge(dve_adjT, s.count(2, plus=2 * T, lag=B_LAG))
                        wait(pe, dve_route, s.div(T, B_LAG))
                        for c in range(C):
                            for t in range(T):
                                for part in range(2):
                                    last = te.matmul(ps_s[:, c:c + 1], x1p[:, b, part, t, c * P:(c + 1) * P],
                                                     ones_h[:, 0:1], start=(t + part == 0),
                                                     stop=(t == T - 1 and part == 1))
                        last.then_inc(pe_mean, 1)
                    wait(pe, act_z, s.count(1, plus=-1, lag=B_LAG))
                    for t in range(T):
                        for i, (left, right) in enumerate(PARTS):
                            last = te.matmul(ps_z[:, s.mod(2, B_LAG), :], x1p[:, b, left, t, k * P:(k + 1) * P],
                                             adjT[:, b, right, t, half * HALF:(half + 1) * HALF],
                                             start=(t + i == 0), stop=(t == T - 1 and i == 2))
                    last.then_inc(pe_z, 1)
                if s.live(C_LAG):
                    half, k = s.mod(T, C_LAG) // 4, s.mod(4, C_LAG)
                    if s.mod(T, C_LAG) == 0:
                        pe.wait_ge(w_landed, s.div(T, C_LAG) * 16 + 16)
                    if k == 0:
                        pe.wait_ge(act_z, s.count(1, plus=4, lag=C_LAG))
                    wait(pe, act_o, s.count(1, lag=C_LAG))
                    for c in range(C):
                        last = te.matmul(ps_o[:], w_sel[:, c, k * P:(k + 1) * P], zT[:, half, c, :],
                                         start=(c == 0), stop=(c == C - 1))
                    last.then_inc(pe_o, 1)
                if s.live():
                    pe.wait_ge(dve_xT, s.count(1, plus=1))
                    wait(pe, dve_y, s.count(1))
                    for c in range(C):
                        for i, (left, right) in enumerate(PARTS):
                            last = te.matmul(ps_h[:], xT[:, s.mod(2), left, c, :], w0T[:, right, c, :],
                                             start=(c + i == 0), stop=(c == C - 1 and i == 2))
                    last.then_inc(pe_h, 1)
                if s.mod(T) == 3 and s.live(T):
                    pe.wait_ge(dve_meanT, s.div(T))
                    for c in range(C):
                        last = te.matmul(ps_s[0:1, 8:8 + E], meanT[:, c:c + 1], rw[:, c, :],
                                         start=(c == 0), stop=(c == C - 1))
                    last.then_inc(pe_score, 1)

            run_slots(pe, body)

            pe.wait_ge(dve_route, NB)
            te.matmul(ps_s[:, 64:64 + NB * E], ones[0:1, :], hot_row[:].rearrange("o b e -> o (b e)"),
                      start=True, stop=True).then_inc(pe_hot, 1)

            def rows(q, i):
                pe.wait_ge(act_relu, q * (4 * C) + (i + 1) * C)
                for t in range(T):
                    wait(pe, dve_y2, q * (4 * T) + (i * T + t - 3))
                    for c in range(C):
                        last = te.transpose(ps_y[t % 4][:, c * P:(c + 1) * P], o_buf[i][:, c, t * P:(t + 1) * P], ident[:])
                    last.then_inc(pe_back, 1)

            run_batches(pe, rows)


_INS = ['x', 'adj', 'L0_gnn_mean_relation', 'L0_gnn_precision_relation', 'L0_gnn_W', 'L1_gnn_router_w',
        'L1_gnn_router_b', 'L1_gnn_expert_w', 'L1_gnn_bn_gamma', 'L1_gnn_bn_beta']


def kernel(**inputs):
    import numpy as _np
    import concourse.bacc as _bacc
    from concourse import mybir as _mybir
    from concourse.bass_utils import run_bass_kernel_spmd as _run

    nc = _bacc.Bacc("TRN2", target_bir_lowering=False, num_devices=1)
    arrays, args = {}, []
    for name in _INS:
        a = _np.ascontiguousarray(inputs[name])
        arrays[f"in_{name}_dram"] = a
        args.append(nc.dram_tensor(f"in_{name}_dram", a.shape, _mybir.dt.from_np(a.dtype), kind="ExternalInput").ap())
    nb, rows, width = inputs['x'].shape
    x1_spill = nc.dram_tensor("x1_spill", (nb, rows, width), F32, kind="Internal").ap()
    out_spill = nc.dram_tensor("out_spill", (nb, width, rows), F32, kind="Internal").ap()
    out = nc.dram_tensor("out_0_dram", (nb, rows, width), F32, kind="ExternalOutput").ap()
    gnn_program(nc, *args, x1_spill, out_spill, out)
    r = _run(nc, [arrays], core_ids=[0])
    return r.results[0]["out_0_dram"]
```

```python
from contextlib import ExitStack

import concourse.bass as bass
from concourse import mybir

ALU = mybir.AluOpType
ACT = mybir.ActivationFunctionType
F32 = mybir.dt.float32
F16 = mybir.dt.float16
I32 = mybir.dt.int32
AX_X = mybir.AxisListType.X

P = 128
LN_EPS = 1e-5
BN_EPS = 1e-5
SUM_SCALE = 2.0 ** 60
X_SCALE = 2.0 ** 4
W0_SCALE = 2.0 ** 8
ADJ_SCALE = 2.0 ** 10
X1_SCALE = 2.0 ** 8
RING = 6
SPAN = 16
B_LAG = 10
C_LAG = 14


class Slot:

    def __init__(self, p, r, total, span=SPAN):
        self.p, self.r, self.total, self.span = p, r, total, span
        self.fixed = isinstance(p, int)

    def live(self, lag=0):
        return not self.fixed or 0 <= self.span * self.p + self.r - lag < self.total

    def mod(self, m, lag=0):
        return (self.r - lag) % m

    def div(self, m, lag=0):
        return self.p * (self.span // m) + (self.r - lag) // m

    def count(self, per=1, plus=0, lag=0):
        return self.p * (self.span * per) + (per * (self.r - lag) + plus)


def wait(eng, sem, value):
    if isinstance(value, int) and value <= 0:
        return
    eng.wait_ge(sem, value)


def held(eng, value):
    return value if isinstance(value, int) else eng.to_reg(value)


def gnn_program(nc, x, adj, mean_rel, prec_rel, w0, router_w, router_b, expert_w, gamma, beta, x1_spill,
                out_spill, out):
    NB, NR, D = x.shape
    NK = mean_rel.shape[0]
    E = expert_w.shape[0]
    T = NR // P
    C = D // P
    G = 4
    HALF = NR // 2
    TILES = NB * T
    KW = D // NK
    assert T == 8 and C == 4 and NK == 4 and HALF == 512 and KW == P and TILES % SPAN == 0

    with ExitStack() as ctx:
        def sb(name, shape, dt=F32):
            return ctx.enter_context(nc.sbuf_tensor(name, shape, dt))

        def sem(name):
            return ctx.enter_context(nc.semaphore(name))

        def sems(name, n):
            return [sem(f"{name}{i}") for i in range(n)]

        adj_in = sb("adj_in", [P, 2, NR])
        x_in = sb("x_in", [P, T, D])
        adjT = sb("adjT", [P, 2, 2, T, NR], F16)
        x1p = sb("x1p", [P, 2, 2, T, D], F16)
        w_sel = sb("w_sel", [P, C, D])
        w0T = sb("w0T", [P, 2, C, D], F16)
        xT = sb("xT", [P, 2, 2, C, P], F16)
        wgt = sb("wgt", [P, 2, NK, NR])
        tot = sb("tot", [P, 2, NR])
        zT = sb("zT", [P, 2, C, HALF])
        o_stage = sb("o_stage", [P, 2, HALF])
        ident = sb("ident", [P, P])
        ones = sb("ones", [1, P])
        ones_h = sb("ones_h", [P, 2], F16)
        neg_mu = sb("neg_mu", [P, NK])
        neg_alpha = sb("neg_alpha", [P, NK])
        eps_x1 = sb("eps_x1", [P, 1])
        eps_bn = sb("eps_bn", [P, 1])
        eps_out = sb("eps_out", [P, 1])
        wsum = sb("wsum", [P, 2, NK])
        y_stat = sb("y_stat", [P, 2, 6])
        y_mv = sb("y_mv", [P, 2, G, 2])
        ln_var = sb("ln_var", [P, G])
        rstd = sb("rstd", [P, 2, G])
        r_mv = sb("r_mv", [P, 4, G, 2])
        r_var = sb("r_var", [P, 4, G])
        r_std = sb("r_std", [P, 4, G])
        r_nmr = sb("r_nmr", [P, 4, G])
        o_stat = sb("o_stat", [P, 2, C, 2, 6])
        o_agg = sb("o_agg", [P, C, 2])
        pad = sb("pad", [P, 1])
        o_mv = sb("o_mv", [P, NB, C, 2])
        rw = sb("rw", [P, C, E])
        rb = sb("rb", [1, E])
        iota_f = sb("iota_f", [1, E])
        iota_i = sb("iota_i", [1, E], I32)
        sumT = sb("sumT", [P, C])
        sc = sb("sc", [1, E])
        sc_max = sb("sc_max", [1, 1])
        sc_idx = sb("sc_idx", [1, 1])
        sc_int = sb("sc_int", [1, 2], I32)
        hot_row = sb("hot_row", [1, NB, E])
        hot = sb("hot", [P, NB, E])
        hot_part = sb("hot_part", [P, NB, E])
        gamT = sb("gamT", [P, E, C])
        betT = sb("betT", [P, E, C])
        e_sum = sb("e_sum", [P, E, 2 * C])
        e_cnt = sb("e_cnt", [P, E])
        e_sq = sb("e_sq", [P, E, C])
        e_lnv = sb("e_lnv", [P, E, C])
        e_scale = sb("e_scale", [P, E, C])
        e_bias = sb("e_bias", [P, E, C])
        b_scale = sb("b_scale", [P, NB, C])
        b_bias = sb("b_bias", [P, NB, C])

        ps_adjT = ctx.enter_context(nc.psum_tensor("ps_adjT", [P, 2, 512], F32))
        ps_xT = ctx.enter_context(nc.psum_tensor("ps_xT", [P, 512], F32))
        ps_h = ctx.enter_context(nc.psum_tensor("ps_h", [P, 512], F32))
        ps_z = ctx.enter_context(nc.psum_tensor("ps_z", [P, 2, 512], F32))
        ps_o = ctx.enter_context(nc.psum_tensor("ps_o", [P, 512], F32))
        ps_s = ctx.enter_context(nc.psum_tensor("ps_s", [P, 512], F32))

        adj_landed = sems("adj_landed", 2)
        x_landed = sems("x_landed", T)
        w_landed = sem("w_landed")
        o_stored = sems("o_stored", 2)
        x1_stored = sems("x1_stored", 2)
        gauss_landed, router_landed = sem("gauss_landed"), sem("router_landed")
        w0_landed = sem("w0_landed")
        bn_landed = sem("bn_landed")
        pe_adjT, pe_xT, pe_h, pe_z, pe_o = (sem(f"pe_{k}") for k in ("adjT", "xT", "h", "z", "o"))
        pe_mean, pe_score, pe_w0, pe_hot, pe_back = (sem(f"pe_{k}") for k in ("mean", "score", "w0", "hot", "back"))
        act_sq, act_w, act_adjT, act_xT = (sem(f"act_{k}") for k in ("sq", "w", "adjT", "xT"))
        act_ln, act_rec, act_z, act_o = (sem(f"act_{k}") for k in ("ln", "rec", "z", "o"))
        act_w0 = sem("act_w0")
        act_lnv, act_rstd, act_bn, act_relu = (sem(f"act_{k}") for k in ("lnv", "rstd", "bn", "relu"))
        act_lnv2, act_rstd2, act_out = (sem(f"act_{k}") for k in ("lnv2", "rstd2", "out"))
        dve_tot, dve_ws, dve_y, dve_stat, dve_mv = (sem(f"dve_{k}") for k in ("tot", "ws", "y", "stat", "mv"))
        dve_x1, dve_ostat, dve_omv, dve_sumT = (sem(f"dve_{k}") for k in ("x1", "ostat", "omv", "sumT"))
        dve_routing, dve_oagg, dve_alpha = sem("dve_routing"), sem("dve_oagg"), sem("dve_alpha")
        dve_route, dve_const, dve_w0, dve_bn = (sem(f"dve_{k}") for k in ("route", "const", "w0", "bn"))
        dve_y2, dve_stat2, dve_mv2 = (sem(f"dve_{k}") for k in ("y2", "stat2", "mv2"))
        pool_nmr = sem("pool_nmr")
        dve_xT, dve_adjT = sem("dve_xT"), sem("dve_adjT")
        pool_const, pool_hi, pool_x1 = sem("pool_const"), sem("pool_hi"), sem("pool_x1")
        o_back, x1_back, y_stored = (sems(name, RING) for name in ("o_back", "x1_back", "y_stored"))

        wgt_flat = wgt[:].rearrange("p a k n -> p (a k n)")
        adjT_flat = adjT[:].rearrange("p a h t n -> p (a h t n)").bitcast(F32)
        x1p_flat = x1p[:].rearrange("p a h t n -> p (a h t n)").bitcast(F32)
        bn_a = o_stage[:, 1, 0:2 * NB * C * E]
        BUF, PART = T * D, T * D // 2

        def halves(flat, at=0):
            return [flat[:, at:at + PART], flat[:, at + PART:at + BUF]]

        areas = [(halves(wgt_flat, BUF), halves(x_in[:].rearrange("p t n -> p (t n)"))),
                 (halves(wgt_flat), halves(adjT_flat)),
                 (halves(adjT_flat, BUF), halves(x1p_flat)),
                 (halves(adjT_flat, 2 * BUF), halves(adjT_flat, 3 * BUF)),
                 (halves(x1p_flat, BUF), halves(zT[:].rearrange("p h c n -> p (h c n)"))),
                 ([tot[:].rearrange("p a n -> p (a n)"), w_sel[:].rearrange("p c n -> p (c n)")],
                  [adj_in[:].rearrange("p a n -> p (a n)"),
                   w0T[:].rearrange("p h c n -> p (h c n)").bitcast(F32)])]
        o_buf = [[part.rearrange("p (c n) -> p c n", c=C // 2) for part in o] for o, _ in areas]
        y_buf = [[part.rearrange("p (t n) -> p t n", t=G) for part in y] for _, y in areas]

        def o_chunk(i, k):
            return o_buf[i][k // 2][:, k % 2, :]

        def y_row(i, t):
            return y_buf[i][t // G][:, t % G, :]

        w0_banks = [ps_z[:, 0, :], ps_z[:, 1, :], ps_o[:], ps_s[:]]
        ps_y = [ps_adjT[:, 0, :], ps_adjT[:, 1, :], ps_xT[:], ps_h[:]]

        PAIRS = TILES // SPAN
        LAST = TILES + C_LAG + 1

        def run_slots(eng, body):
            for r in range(SPAN):
                body(Slot(0, r, TILES))
            with eng.Fori(1, PAIRS) as p:
                for r in range(SPAN):
                    body(Slot(p, r, TILES))
            for n in range(TILES, LAST):
                body(Slot(PAIRS, n - TILES, TILES))

        def run_steps(body, last):
            for n in range(NB + last):
                body(Slot(0, n, NB, NB))

        def batch_of(s, lag=0):
            n = s.r - lag
            return NB - 1 - n if n < 2 else n - 2

        def landed(sems_, s, lag=0):
            return sems_[s.mod(RING, lag)], s.div(RING, lag) * 32 + (32 if s.mod(RING, lag) else 0)

        def kept(s):
            return s.fixed and s.p == PAIRS

        def ps_out(s, lag):
            return ps_h if second_bank(s, lag) else ps_o

        def second_bank(s, lag):
            return s.fixed and s.p == PAIRS and s.r > lag - C_LAG and s.mod(2, lag) == 1

        def out_unit(s):
            half, k = s.mod(T, C_LAG + 1) // 4, s.mod(4, C_LAG + 1)
            if kept(s):
                pair = 0 if s.div(T, C_LAG + 1) == NB - 1 else 1
                return o_chunk(pair, k)[:, half * HALF:(half + 1) * HALF]
            return o_stage[:, k % 2, :]

        BN_VAR, BN_DONE = 12, 19

        block = ctx.enter_context(nc.Block())

        @block.sync
        def _(sp):
            sp.dma_start(neg_mu[:], mean_rel.rearrange("(o k) -> o k", o=1).broadcast_to([P, NK])).then_inc(gauss_landed, 16)
            sp.dma_start(neg_alpha[:], prec_rel.rearrange("(o k) -> o k", o=1).broadcast_to([P, NK])).then_inc(gauss_landed, 16)

            def load_adj(s, ahead):
                squared = held(sp, s.count(4, plus=4 * (ahead - 1)))
                transposed = held(sp, s.count(2, plus=2 * (ahead - 1)))
                wait(sp, act_sq, squared)
                wait(sp, pe_adjT, transposed)
                k = s.mod(2, -ahead)
                src = adj.rearrange("b (t p) n -> (b t) p n", p=P)[s.count(1, plus=ahead)]
                sp.dma_start(adj_in[:, k, :], src).then_inc(adj_landed[k], 16)

            def load_x(s, ahead):
                if s.mod(G, T - ahead) == 0 and s.live(T - ahead):
                    split = held(sp, s.count(1, plus=G, lag=T - ahead))
                    stored = held(sp, s.div(T, T - ahead) * 16 + 16)
                    wait(sp, pool_x1, split)
                    wait(sp, x1_stored[s.mod(T, T - ahead) // G], stored)
                k = s.mod(T, -ahead)
                src = x.rearrange("b (t p) n -> (b t) p n", p=P)[s.count(1, plus=ahead)]
                sp.dma_start(x_in[:, k, :], src).then_inc(x_landed[k], 16)

            for k in range(2):
                sp.dma_start(adj_in[:, k, :], adj[0, k * P:(k + 1) * P, :]).then_inc(adj_landed[k], 16)
                sp.dma_start(x_in[:, k, :], x[0, k * P:(k + 1) * P, :]).then_inc(x_landed[k], 16)
                if k == 0:
                    sp.dma_start(wgt[:, 1, :, 0:D], w0.rearrange("n o d -> o n d")).then_inc(w0_landed, 16)
            sp.dma_start(rw[:], router_w.rearrange("(c p) e -> p c e", p=P)).then_inc(router_landed, 16)
            sp.dma_start(rb[:], router_b.rearrange("(o e) -> o e", o=1)).then_inc(router_landed, 16)

            def body(s):
                fetch = s.mod(T, C_LAG) == 0 and s.live(C_LAG)
                if fetch:
                    routed = held(sp, s.div(T, C_LAG) + 1)
                    used = held(sp, s.count(1, lag=C_LAG))
                    wait(sp, dve_route, routed)
                    wait(sp, pe_o, used)
                if s.live(-2):
                    load_x(s, 2)
                if fetch:
                    m = s.mod(2 * T, C_LAG) // T
                    e = sp.value_load(sc_int[0:1, m:m + 1], min_val=0, max_val=E - 1)
                    sp.dma_start(w_sel[:], expert_w.rearrange("e (c p) k -> e p c k", p=P)[e]).then_inc(w_landed, 16)
                if s.live(-2):
                    load_adj(s, 2)

            for r in range(SPAN):
                body(Slot(0, r, TILES))
            with sp.Fori(1, PAIRS - 1) as p:
                for r in range(SPAN):
                    body(Slot(p, r, TILES))
            for n in range(TILES - SPAN, LAST):
                body(Slot(n // SPAN, n % SPAN, TILES))

            def last_pass(s):
                n, b = s.r, batch_of(s)
                i = s.mod(RING)
                if n == 1:
                    sp.wait_ge(o_stored[0], (TILES - 2 * T) * 8 + 16)
                    sp.wait_ge(dve_ws, NK * (TILES - 1))
                    for part in (slice(0, HALF // 2), slice(HALF // 2, HALF)):
                        sp.dma_start(o_chunk(i, 0)[:, part], out_spill[b, 0:P, part]).then_inc(o_back[i], 16)
                elif 1 < n < NB:
                    if n < RING:
                        sp.wait_ge(pe_z, TILES - T if n == 2 else TILES)
                        if n == 5:
                            sp.wait_ge(dve_ws, NK * TILES)
                            sp.wait_ge(pe_o, TILES)
                    else:
                        sp.wait_ge(pe_back, (n - RING + 1) * T)
                        wait(sp, *landed(o_back, s, RING))
                    for k in range(2):
                        sp.wait_ge(o_stored[k], (b + 1) * T * 8)
                    for h in range(2):
                        src = out_spill.rearrange("b (h c p) n -> b h p c n", h=2, p=P)[b, h]
                        sp.dma_start(o_buf[i][h], src).then_inc(o_back[i], 16)
                if s.live(RING):
                    for g in range(2):
                        sp.wait_ge(act_out, s.count(T, plus=(g + 1) * G, lag=RING))
                        dst = out.rearrange("b (g t p) n -> b g p t n", g=2, p=P)[batch_of(s, RING), g]
                        sp.dma_start(dst, y_buf[i][g]).then_inc(y_stored[i], 16)
                if 0 < n < NB:
                    if n >= RING:
                        sp.wait_ge(y_stored[i], 32)
                        wait(sp, *landed(x1_back, s, RING))
                    elif n == 4:
                        sp.wait_ge(pe_o, TILES)
                    elif n == 5:
                        sp.wait_ge(act_sq, NK * TILES)
                        sp.wait_ge(pe_adjT, 2 * TILES)
                        sp.wait_ge(pe_h, TILES)
                    elif n == 1:
                        sp.wait_ge(pe_z, TILES - T)
                    for k in range(2):
                        sp.wait_ge(x1_stored[k], (b + 1) * 16)
                    for g in range(2):
                        src = x1_spill.rearrange("b (g t p) n -> b g p t n", g=2, p=P)[b, g]
                        sp.dma_start(y_buf[i][g], src).then_inc(x1_back[i], 16)

            run_steps(last_pass, RING)
            for i in range(RING):
                sp.wait_ge(y_stored[i], len(range(i, NB, RING)) * 32)

        @block.gpsimd
        def _(pool):
            nc.gpsimd.memset(ident[:], 0.0).then_inc(pool_const, 1)
            pool.wait_ge(pool_const, 1)
            nc.gpsimd.affine_select(out=ident[:], in_=ident[:], compare_op=ALU.not_equal, fill=1.0, base=0,
                                    pattern=[[-1, P]], channel_multiplier=1).then_inc(pool_const, 1)
            nc.gpsimd.iota(iota_i[:], pattern=[[1, E]], base=0, channel_multiplier=0).then_inc(pool_const, 1)
            with nc.allow_non_contiguous_dma("two small transposed tables"):
                for k in range(C):
                    pool.dma_start(gamT[:, :, k], gamma[:, k * P:(k + 1) * P].rearrange("e p -> p e")).then_inc(bn_landed, 16)
                    pool.dma_start(betT[:, :, k], beta[:, k * P:(k + 1) * P].rearrange("e p -> p e")).then_inc(bn_landed, 16)

            def body(s):
                if s.mod(G) == 1 and s.live(G + 1):
                    pool.wait_ge(dve_x1, s.count(1, lag=1))
                    g = s.mod(SPAN, G + 1) // G
                    h, m = g % 2, g // 2
                    if h == 0:
                        wait(pool, pe_z, s.count(1, plus=-T, lag=G + 1))
                    if not (s.fixed and s.p == PAIRS):
                        dst = x1_spill.rearrange("b (g t p) n -> (b g) p t n", g=2, p=P)[s.div(G, G + 1)]
                        pool.dma_start(dst, x_in[:, h * G:(h + 1) * G, :]).then_inc(x1_stored[h], 16)
                    for t in range(h * G, (h + 1) * G):
                        nc.gpsimd.tensor_scalar(x1p[:, m, 0, t, :], x_in[:, t, :], 1.0, 1.0, ALU.mult,
                                                ALU.mult).then_inc(pool_hi, 1)
                        pool.wait_ge(pool_hi, s.count(1, plus=t - h * G + 1, lag=G + 1))
                        nc.gpsimd.tensor_tensor(x1p[:, m, 1, t, :], x_in[:, t, :], x1p[:, m, 0, t, :],
                                                ALU.subtract).then_inc(pool_x1, 1)
                if s.live(C_LAG + 1) and not kept(s):
                    pool.wait_ge(act_o, s.count(1, plus=1, lag=C_LAG + 1))
                    k = s.mod(4, C_LAG + 1)
                    half = s.mod(T, C_LAG + 1) // 4
                    dst = out_spill.rearrange("b (c p) n -> b c p n", p=P)[
                        s.div(T, C_LAG + 1), k, :, half * HALF:(half + 1) * HALF]
                    pool.dma_start(dst, o_stage[:, k % 2, :]).then_inc(o_stored[k % 2], 16)

            run_slots(pool, body)

            def shifts(s):
                for g in range(2):
                    r = s.mod(2) * 2 + g
                    pool.wait_ge(act_rstd2, s.count(2, plus=g + 1))
                    wait(pool, act_out, s.count(T, plus=g * G, lag=2) + G)
                    nc.gpsimd.tensor_tensor(r_nmr[:, r, :], r_mv[:, r, :, 0], r_std[:, r, :], ALU.mult).then_inc(pool_nmr, 1)
                    pool.wait_ge(pool_nmr, s.count(4, plus=2 * g + 1))
                    nc.gpsimd.tensor_scalar(r_nmr[:, r, :], r_nmr[:, r, :], -1.0, 1.0, ALU.mult, ALU.mult).then_inc(pool_nmr, 1)

            run_steps(shifts, 0)

        @block.scalar
        def _(act):
            nc.scalar.preload_act_table_set("natural_log_exp_and_others")
            act.wait_ge(dve_const, 2)

            def body(s):
                if s.live(C_LAG + 1):
                    k = s.mod(4, C_LAG + 1)
                    act.wait_ge(pe_o, s.count(1, plus=1, lag=C_LAG + 1))
                    if kept(s):
                        act.wait_ge(dve_ws, NK * (TILES if s.div(T, C_LAG + 1) == NB - 1 else TILES - 1))
                    else:
                        wait(act, o_stored[k % 2], s.div(2, C_LAG + 1) * 16)
                        wait(act, dve_ostat, s.count(1, lag=C_LAG + 1))
                    nc.scalar.activation(out_unit(s), ps_out(s, C_LAG + 1)[:], ACT.Copy).then_inc(act_o, 1)
                def sum_reciprocal():
                    if s.live(1):
                        j = s.mod(2, 1)
                        act.wait_ge(dve_tot, s.count(3))
                        nc.scalar.activation(tot[:, j, :], tot[:, j, :], ACT.Ln, scale=SUM_SCALE).then_inc(act_ln, 1)
                        act.wait_ge(act_ln, s.count(1))
                        nc.scalar.activation(tot[:, j, :], tot[:, j, :], ACT.Exp, scale=-1.0).then_inc(act_rec, 1)

                if not s.live():
                    sum_reciprocal()
                if s.live():
                    a, m = s.mod(2), s.mod(2)
                    act.wait_ge(adj_landed[a], s.div(2) * 16 + 16)
                    wait(act, dve_ws, s.count(NK, plus=-NK))
                    if s.fixed and s.p == 0 and s.r == 1:
                        act.wait_ge(pe_w0, C)
                    def square(k):
                        nc.scalar.activation(wgt[:, m, k, :], adj_in[:, a, :], ACT.Square,
                                             bias=neg_mu[:, k:k + 1]).then_inc(act_sq, 1)

                    def weigh(k):
                        act.wait_ge(act_sq, s.count(4, plus=k + 1))
                        nc.scalar.activation(wgt[:, m, k, :], wgt[:, m, k, :], ACT.Exp,
                                             scale=neg_alpha[:, k:k + 1]).then_inc(act_w, 1)

                    square(0)
                    sum_reciprocal()
                    square(1)
                    act.wait_ge(pe_xT, s.count(1, plus=1))
                    wait(act, pe_h, s.count(1, plus=-1))
                    nc.scalar.activation(xT[:, m, 0, :, :].rearrange("p c n -> p (c n)"), ps_xT[:],
                                         ACT.Copy, scale=X_SCALE).then_inc(act_xT, 1)
                    weigh(0)
                    weigh(1)
                    square(2)
                    square(3)
                    weigh(2)
                    weigh(3)
                    b, t = s.mod(2 * T) // T, s.mod(T)
                    if t % 4 == 0:
                        wait(act, pe_z, s.count(1, plus=-12))
                    for h in range(2):
                        act.wait_ge(pe_adjT, s.count(2, plus=h + 1))
                        nc.scalar.activation(adjT[:, b, 0, 4 * h:4 * h + 4, t * P:(t + 1) * P],
                                             ps_adjT[:, h, :].rearrange("p (c n) -> p c n", c=4),
                                             ACT.Copy, scale=ADJ_SCALE).then_inc(act_adjT, 1)
                if s.fixed and s.p == 0 and s.r == 0:
                    for c in range(C):
                        act.wait_ge(pe_w0, c + 1)
                        nc.scalar.activation(w0T[:, 0, c, :], w0_banks[c], ACT.Copy, scale=W0_SCALE).then_inc(act_w0, 1)
                if s.live(B_LAG):
                    u, half, k = s.mod(2, B_LAG), s.mod(T, B_LAG) // 4, s.mod(4, B_LAG)
                    act.wait_ge(pe_z, s.count(1, plus=1, lag=B_LAG))
                    if k == 0:
                        wait(act, pe_o, s.count(1, plus=-4, lag=B_LAG))
                    nc.scalar.activation(zT[:, half, k, :], ps_z[:, u, :], ACT.Copy,
                                         scale=1.0 / (ADJ_SCALE * X1_SCALE)).then_inc(act_z, 1)
                if s.mod(G) == 0 and s.live(G):
                    g = s.mod(2 * G, G) // G
                    act.wait_ge(dve_mv, s.count(1))
                    nc.scalar.activation(ln_var[:], y_mv[:, g, :, 1], ACT.Ln, bias=eps_x1[:, 0:1],
                                         scale=X1_SCALE ** -2).then_inc(act_lnv, 1)
                    act.wait_ge(act_lnv, s.div(G))
                    nc.scalar.activation(rstd[:, g, :], ln_var[:], ACT.Exp, scale=-0.5).then_inc(act_rstd, 1)

            run_slots(act, body)

            act.wait_ge(dve_bn, BN_VAR)
            nc.scalar.activation(e_lnv[:], e_sq[:], ACT.Ln, bias=eps_bn[:, 0:1]).then_inc(act_bn, 1)
            act.wait_ge(act_bn, 1)
            nc.scalar.activation(e_scale[:], e_lnv[:], ACT.Exp, scale=-0.5).then_inc(act_bn, 1)
            act.wait_ge(dve_bn, BN_DONE)

            def relu(s, chunks):
                if s.live():
                    i = s.mod(RING)
                    if chunks[0] == 0:
                        wait(act, act_o, TILES if s.r < 2 else 0)
                        wait(act, *landed(o_back, s))
                    parts = [slice(0, NR)]
                    if s.r == 0:
                        chunks = range(C) if chunks[0] == 0 else ()
                        parts = [slice(0, HALF), slice(HALF, NR)]
                    for part in parts:
                        for k in chunks:
                            nc.scalar.activation(o_chunk(i, k)[:, part], o_chunk(i, k)[:, part], ACT.Relu,
                                                 bias=b_bias[:, batch_of(s), k:k + 1],
                                                 scale=b_scale[:, batch_of(s), k:k + 1]).then_inc(act_relu, 1)

            def scales(s, lag, g):
                if s.live(lag):
                    r = s.mod(2, lag) * 2 + g
                    act.wait_ge(dve_mv2, s.count(T, plus=(g + 1) * G, lag=lag))
                    nc.scalar.activation(r_var[:, r, :], r_mv[:, r, :, 1], ACT.Ln, bias=eps_out[:, 0:1]).then_inc(act_lnv2, 1)
                    act.wait_ge(act_lnv2, s.count(2, plus=g + 1, lag=lag))
                    nc.scalar.activation(r_std[:, r, :], r_var[:, r, :], ACT.Exp, scale=-0.5).then_inc(act_rstd2, 1)

            def norm(s, lag, g, tiles):
                if s.live(lag):
                    i, r = s.mod(RING, lag), s.mod(2, lag) * 2 + g
                    act.wait_ge(pool_nmr, s.count(4, plus=2 * g + 2, lag=lag))
                    for t in tiles:
                        row = y_row(i, g * G + t)
                        nc.scalar.activation(row, row, ACT.Identity, bias=r_nmr[:, r, t:t + 1],
                                             scale=r_std[:, r, t:t + 1]).then_inc(act_out, 1)

            def rows(s):
                relu(s, (0, 1))
                scales(s, 2, 1)
                relu(s, (2, 3))
                norm(s, 2, 1, range(0, 3))
                scales(s, 1, 0)
                norm(s, 2, 1, range(3, 4))
                norm(s, 1, 0, range(0, 4))

            run_steps(rows, 2)


        @block.vector
        def _(dve):
            v = nc.vector
            v.memset(ones[:], 1.0).then_inc(dve_ostat, 1)
            v.memset(ones_h[:], 1.0)
            v.memset(eps_x1[:], LN_EPS * X1_SCALE ** -2)
            v.memset(eps_bn[:], BN_EPS)
            v.memset(eps_out[:], LN_EPS * X1_SCALE ** 2)
            dve.wait_ge(gauss_landed, 32)
            v.tensor_tensor(neg_alpha[:], neg_alpha[:], neg_alpha[:], ALU.mult).then_inc(dve_alpha, 1)
            dve.wait_ge(dve_alpha, 1)
            v.tensor_scalar(neg_alpha[:], neg_alpha[:], 1e-14, -2.0, ALU.add, ALU.mult).then_inc(dve_alpha, 1)
            dve.wait_ge(dve_alpha, 2)
            v.reciprocal(neg_alpha[:], neg_alpha[:]).then_inc(dve_const, 1)
            v.tensor_scalar(neg_mu[:], neg_mu[:], -1.0, None, ALU.mult).then_inc(dve_const, 1)

            def split_w0():
                for c in range(C):
                    dve.wait_ge(act_w0, c + 1)
                    v.scalar_tensor_tensor(out=w0T[:, 1, c, :], in0=w0_banks[c], scalar=W0_SCALE, in1=w0T[:, 0, c, :],
                                           op0=ALU.mult, op1=ALU.subtract).then_inc(dve_w0, 1)
                dve.wait_ge(router_landed, 32)
                dve.wait_ge(pool_const, 3)
                v.tensor_copy(iota_f[:], iota_i[:]).then_inc(dve_w0, 1)

            done = [0]

            def then(ins):
                done[0] += 1
                ins.then_inc(dve_bn, 1)
                dve.wait_ge(dve_bn, done[0])

            def expert_shares():
                dve.wait_ge(pe_hot, 1)
                then(v.tensor_copy(hot[:], ps_s[:, 64:64 + NB * E].rearrange("p (b e) -> p b e", b=NB)))
                then(v.tensor_reduce(e_cnt[:], hot[:].rearrange("p b e -> p e b"), AX_X, ALU.add))
                then(v.tensor_scalar(e_cnt[:], e_cnt[:], 1.0 / NR, None, ALU.max))
                then(v.reciprocal(e_cnt[:], e_cnt[:]))
                for b in range(NB):
                    last = v.tensor_tensor(hot_part[:, b, :], hot[:, b, :], e_cnt[:], ALU.mult)
                then(last)
                dve.wait_ge(bn_landed, 16 * 2 * C)
                v.tensor_scalar(betT[:], betT[:], X1_SCALE, None, ALU.mult)
                then(v.tensor_scalar(gamT[:], gamT[:], X1_SCALE, None, ALU.mult))

            def body(s):
                def route(k):
                    if s.mod(T) != 4 or not s.live(T):
                        return
                    m = s.mod(2 * T, T) // T
                    if k == 0:
                        dve.wait_ge(pe_score, s.div(T))
                        step = v.scalar_tensor_tensor(out=sc[:], in0=ps_s[0:1, 8:8 + E], scalar=1.0 / (NR * X1_SCALE),
                                                      in1=rb[:], op0=ALU.mult, op1=ALU.add)
                    else:
                        dve.wait_ge(dve_routing, s.div(T) * 5 + (k - 5))
                    if k == 1:
                        step = v.reduce_max(sc_max[:], sc[:], AX_X)
                    if k == 2:
                        step = v.tensor_scalar(sc[:], sc[:], sc_max[0:1, 0:1], float(E), ALU.is_lt, ALU.mult)
                    if k == 3:
                        step = v.tensor_tensor(sc[:], sc[:], iota_f[:], ALU.add)
                    if k == 4:
                        step = v.tensor_reduce(sc_idx[:], sc[:], AX_X, ALU.min)
                    if k < 5:
                        step.then_inc(dve_routing, 1)
                    else:
                        v.tensor_copy(sc_int[0:1, m:m + 1], sc_idx[:])
                        hot_at = hot_row[:].rearrange("o b e -> o (b e)")[:, bass.ds(s.div(T) * E - E, E)]
                        v.tensor_scalar(hot_at, iota_f[:], sc_idx[0:1, 0:1], None, ALU.is_equal).then_inc(dve_route, 1)

                def y_stats():
                    if s.live(1):
                        dve.wait_ge(dve_y, s.count(1))
                        v.bn_stats(y_stat[:, s.mod(2, 1), :], x_in[:, s.mod(T, 1), :]).then_inc(dve_stat, 1)

                def y_mean_var():
                    if s.live(1):
                        v.bn_aggr(y_mv[:, s.mod(2 * G, 1) // G, s.mod(G, 1), :], y_stat[:, s.mod(2, 1), :]).then_inc(dve_mv, 1)

                m = s.mod(2)
                if s.live():
                    dve.wait_ge(act_w, s.count(4, plus=2))
                    v.tensor_tensor(tot[:, m, :], wgt[:, m, 0, :], wgt[:, m, 1, :], ALU.add).then_inc(dve_tot, 1)
                    dve.wait_ge(act_xT, s.count(1, plus=1))
                    v.scalar_tensor_tensor(out=xT[:, m, 1, :, :].rearrange("p c n -> p (c n)"), in0=ps_xT[:],
                                           scalar=X_SCALE, in1=xT[:, m, 0, :, :].rearrange("p c n -> p (c n)"),
                                           op0=ALU.mult, op1=ALU.subtract).then_inc(dve_xT, 1)
                early = s.mod(G) == 0 and s.live()
                if early:
                    y_stats()
                if s.live():
                    dve.wait_ge(act_w, s.count(4, plus=3))
                    dve.wait_ge(dve_tot, s.count(3, plus=1))
                    if early and s.live(1):
                        dve.wait_ge(dve_stat, s.count(1))
                    v.tensor_tensor(tot[:, m, :], tot[:, m, :], wgt[:, m, 2, :], ALU.add).then_inc(dve_tot, 1)
                    if early:
                        y_mean_var()
                    dve.wait_ge(act_w, s.count(4, plus=4))
                    dve.wait_ge(dve_tot, s.count(3, plus=2))
                    v.tensor_tensor(tot[:, m, :], tot[:, m, :], wgt[:, m, 3, :], ALU.add).then_inc(dve_tot, 1)
                if s.live():
                    b, t = s.mod(2 * T) // T, s.mod(T)
                    for h in range(2):
                        dve.wait_ge(act_adjT, s.count(2, plus=h + 1))
                        v.scalar_tensor_tensor(out=adjT[:, b, 1, 4 * h:4 * h + 4, t * P:(t + 1) * P],
                                               in0=ps_adjT[:, h, :].rearrange("p (c n) -> p c n", c=4), scalar=ADJ_SCALE,
                                               in1=adjT[:, b, 0, 4 * h:4 * h + 4, t * P:(t + 1) * P],
                                               op0=ALU.mult, op1=ALU.subtract).then_inc(dve_adjT, 1)
                if s.fixed and s.p == 0 and s.r == 0:
                    split_w0()
                if s.fixed and s.p == PAIRS and s.r == 6:
                    expert_shares()
                if not early:
                    y_stats()
                if s.live(C_LAG + 1):
                    half, k = s.mod(T, C_LAG + 1) // 4, s.mod(4, C_LAG + 1)
                    m = s.mod(2 * T, C_LAG + 1) // T
                    dve.wait_ge(act_o, s.count(1, plus=1, lag=C_LAG + 1))
                    v.bn_stats(o_stat[:, m, k, half, :], out_unit(s)).then_inc(dve_ostat, 1)
                    if half == 1 and k == 3:
                        dve.wait_ge(dve_ostat, s.count(1, plus=2, lag=C_LAG + 1))
                        v.memset(pad[:], 0.0)
                        for c in range(C):
                            last = v.bn_aggr(o_agg[:, c, :], o_stat[:, m, c, :, :].rearrange("p h s -> p (h s)"))
                        last.then_inc(dve_oagg, 1)
                        dve.wait_ge(dve_oagg, s.div(T, C_LAG + 1) + 1)
                        v.tensor_copy(o_mv[:].rearrange("p b c s -> p (b c s)")[
                            :, bass.ds(s.div(T, C_LAG + 1) * (2 * C), 2 * C)],
                            o_agg[:].rearrange("p c s -> p (c s)")).then_inc(dve_omv, 1)
                if not early and s.live(1):
                    dve.wait_ge(dve_stat, s.count(1))
                    v.memset(pad[:], 0.0)
                    y_mean_var()
                if s.mod(G) == 0 and s.live(G):
                    g, h = s.mod(2 * G, G) // G, s.mod(T, G) // G
                    dve.wait_ge(dve_mv, s.count(1))
                    dve.wait_ge(act_rstd, s.div(G))
                    for t in range(G):
                        row = x_in[:, h * G + t, :]
                        v.tensor_scalar(row, row, y_mv[:, g, t, 0:1], rstd[:, g, t:t + 1],
                                        ALU.subtract, ALU.mult).then_inc(dve_x1, 1)
                if s.mod(T) == 3 and s.live(T):
                    dve.wait_ge(pe_mean, s.div(T))
                    v.tensor_copy(sumT[:], ps_s[:, 0:C]).then_inc(dve_sumT, 1)
                    dve.wait_ge(dve_sumT, s.div(T) * 2 - 1)
                    v.tensor_tensor(sumT[:], sumT[:], ps_s[:, C:2 * C], ALU.add).then_inc(dve_sumT, 1)
                if s.live():
                    j, t = s.mod(2), s.mod(T)
                    dve.wait_ge(act_rec, s.count(1, plus=1))
                    for k in range(NK):
                        v.scalar_tensor_tensor(out=wgt[:, j, k, :], in0=wgt[:, j, k, :],
                                               scalar=SUM_SCALE / (X_SCALE * W0_SCALE), in1=tot[:, j, :],
                                               op0=ALU.mult, op1=ALU.mult,
                                               accum_out=wsum[:, j, k:k + 1]).then_inc(dve_ws, 1)
                        route(k)
                    dve.wait_ge(pe_h, s.count(1, plus=1))
                    dve.wait_ge(x_landed[t], s.div(T) * 16 + 16)
                    for k in range(NK):
                        f = slice(k * KW, (k + 1) * KW)
                        dve.wait_ge(dve_ws, s.count(NK, plus=k + 1))
                        v_y = v.scalar_tensor_tensor(out=x_in[:, t, f], in0=ps_h[:, f], scalar=wsum[:, j, k:k + 1],
                                                     in1=x_in[:, t, f], op0=ALU.mult, op1=ALU.add)
                        if k % 2 == 0:
                            route(4 + k // 2)
                    v_y.then_inc(dve_y, 1)
                else:
                    for k in range(6):
                        route(k)

            run_slots(dve, body)

            dve.wait_ge(dve_omv, NB)
            dve.wait_ge(o_stored[1], (TILES - 2 * T) * 8)
            mean = o_mv[:, :, :, 0]
            then(v.tensor_tensor(bn_a[:, 0:NB * C].rearrange("p (b c) -> p b c", b=NB), mean, mean, ALU.mult))
            then(v.tensor_tensor(o_mv[:, :, :, 1], o_mv[:, :, :, 1],
                                 bn_a[:, 0:NB * C].rearrange("p (b c) -> p b c", b=NB), ALU.add))
            for e in range(E):
                prod = bn_a[:, e * NB * C * 2:(e + 1) * NB * C * 2].rearrange("p (k b) -> p k b", b=NB)
                last = v.tensor_tensor(prod, o_mv[:].rearrange("p b c s -> p (c s) b"),
                                       hot_part[:, :, e].rearrange("p (o b) -> p o b", o=1).broadcast_to([P, 2 * C, NB]),
                                       ALU.mult)
            then(last)
            then(v.tensor_reduce(e_sum[:].rearrange("p e k -> p (e k)"), bn_a.rearrange("p (k b) -> p k b", b=NB),
                                 AX_X, ALU.add))
            e_mean = e_sum[:].rearrange("p e (c s) -> p e c s", s=2)[:, :, :, 0]
            e_msq = e_sum[:].rearrange("p e (c s) -> p e c s", s=2)[:, :, :, 1]
            then(v.tensor_tensor(e_bias[:], e_mean, e_mean, ALU.mult))
            then(v.tensor_tensor(e_sq[:], e_msq, e_bias[:], ALU.subtract))
            assert done[0] == BN_VAR
            dve.wait_ge(act_bn, 2)
            then(v.tensor_tensor(e_scale[:], e_scale[:], gamT[:], ALU.mult))
            then(v.tensor_tensor(e_bias[:], e_mean, e_scale[:], ALU.mult))
            then(v.tensor_tensor(e_bias[:], betT[:], e_bias[:], ALU.subtract))
            for e_val, b_val in ((e_scale, b_scale), (e_bias, b_bias)):
                for c in range(C):
                    last = v.tensor_tensor(bn_a[:, c * NB * E:(c + 1) * NB * E].rearrange("p (b e) -> p b e", b=NB),
                                           hot[:], e_val[:, :, c].rearrange("p (o e) -> p o e", o=1)
                                           .broadcast_to([P, NB, E]), ALU.mult)
                then(last)
                then(v.tensor_reduce(b_val[:].rearrange("p b c -> p c b"),
                                     bn_a[:, 0:C * NB * E].rearrange("p (c b e) -> p c b e", c=C, b=NB),
                                     AX_X, ALU.add))
            assert done[0] == BN_DONE

            def rows(s):
                for t in range(T):
                    if s.live():
                        if t == 0:
                            if s.r == 0:
                                dve.wait_ge(dve_x1, TILES)
                                dve.wait_ge(x1_stored[0], NB * 16)
                            wait(dve, *landed(x1_back, s))
                        row = y_row(s.mod(RING), t)
                        dve.wait_ge(pe_back, s.count(T, plus=t + 1))
                        v.tensor_tensor(row, ps_y[t % 4], row, ALU.add).then_inc(dve_y2, 1)
                    one, two = (1 if t < 1 else 0), (1 if t < 2 else 0)
                    if s.live(two):
                        dve.wait_ge(dve_stat2, s.count(T, plus=t - 1))
                        if (t - 2) % G == 0:
                            wait(dve, act_out, s.count(T, plus=t - 2 - 3 * G))
                    if s.live(one):
                        dve.wait_ge(dve_y2, s.count(T, plus=t))
                        wait(dve, dve_mv2, s.count(T, plus=t - 2))
                        v.bn_stats(y_stat[:, (t - 1) % 2, :], y_row(s.mod(RING, one), (t - 1) % T)).then_inc(dve_stat2, 1)
                    elif s.live(two):
                        v.memset(pad[:], 0.0)
                    if s.live(two):
                        v.bn_aggr(r_mv[:, s.mod(2, two) * 2 + (t - 2) % T // G, (t - 2) % G, :], y_stat[:, t % 2, :]).then_inc(dve_mv2, 1)
                    if not s.live() and t == 1:
                        return

            run_steps(rows, 1)

        @block.tensor
        def _(pe):
            te = nc.tensor
            PARTS = ((0, 0), (0, 1), (1, 0))
            pe.wait_ge(pool_const, 2)

            def transpose_w0():
                pe.wait_ge(w0_landed, 16)
                for c in range(C):
                    for n in range(NK):
                        last = te.transpose(w0_banks[c][:, n * P:(n + 1) * P], wgt[:, 1, n, c * P:(c + 1) * P], ident[:])
                    last.then_inc(pe_w0, 1)

            def transposes(s):
                a = s.mod(2)
                pe.wait_ge(adj_landed[a], s.div(2) * 16 + 16)
                for h in range(2):
                    wait(pe, dve_adjT, s.count(2, plus=h - 1))
                    for c in range(4):
                        j = 4 * h + c
                        last = te.transpose(ps_adjT[:, h, c * P:(c + 1) * P], adj_in[:, a, j * P:(j + 1) * P], ident[:])
                    last.then_inc(pe_adjT, 1)
                pe.wait_ge(x_landed[s.mod(T)], s.div(T) * 16 + 16)
                wait(pe, dve_xT, s.count(1))
                for c in range(C):
                    last = te.transpose(ps_xT[:, c * P:(c + 1) * P], x_in[:, s.mod(T), c * P:(c + 1) * P], ident[:])
                last.then_inc(pe_xT, 1)

            def mean(b, half):
                for c in range(C):
                    for t in range(half * G, (half + 1) * G):
                        for part in range(2):
                            at = half * C + c
                            last = te.matmul(ps_s[:, at:at + 1], x1p[:, b, part, t, c * P:(c + 1) * P], ones_h[:, 0:1],
                                             start=(t % G + part == 0), stop=(t % G == G - 1 and part == 1))
                return last

            def body(s):
                first = s.fixed and s.p == 0
                if s.live() and not (first and s.r == 1):
                    transposes(s)
                if first and s.r == 0:
                    transpose_w0()
                    transposes(Slot(0, 1, TILES))
                    pe.wait_ge(dve_w0, C + 1)
                if s.mod(T, B_LAG - G) == 0 and s.live(B_LAG - G):
                    pe.wait_ge(pool_x1, s.count(1, plus=G, lag=B_LAG - G))
                    wait(pe, dve_route, s.div(T, B_LAG - G))
                    mean(s.mod(2 * T, B_LAG - G) // T, 0)
                if s.fixed and s.p == PAIRS and s.r == 5:
                    pe.wait_ge(dve_route, NB)
                    te.matmul(ps_s[:, 64:64 + NB * E], ones[0:1, :], hot_row[:].rearrange("o b e -> o (b e)"),
                              start=True, stop=True).then_inc(pe_hot, 1)
                if s.mod(T) == 4 and s.live(T):
                    pe.wait_ge(dve_sumT, s.div(T) * 2)
                    for c in range(C):
                        last = te.matmul(ps_s[0:1, 8:8 + E], sumT[:, c:c + 1], rw[:, c, :],
                                         start=(c == 0), stop=(c == C - 1))
                    last.then_inc(pe_score, 1)
                if s.live(B_LAG):
                    b, half, k = s.mod(2 * T, B_LAG) // T, s.mod(T, B_LAG) // 4, s.mod(4, B_LAG)
                    if s.mod(T, B_LAG) == 0:
                        pe.wait_ge(pool_x1, s.count(1, plus=T, lag=B_LAG))
                        pe.wait_ge(dve_adjT, s.count(2, plus=2 * T, lag=B_LAG))
                        mean(b, 1).then_inc(pe_mean, 1)
                    wait(pe, act_z, s.count(1, plus=-1, lag=B_LAG))
                    for t in range(T):
                        for i, (left, right) in enumerate(PARTS):
                            last = te.matmul(ps_z[:, s.mod(2, B_LAG), :], x1p[:, b, left, t, k * P:(k + 1) * P],
                                             adjT[:, b, right, t, half * HALF:(half + 1) * HALF],
                                             start=(t + i == 0), stop=(t == T - 1 and i == 2))
                    last.then_inc(pe_z, 1)
                if s.live(C_LAG):
                    half, k = s.mod(T, C_LAG) // 4, s.mod(4, C_LAG)
                    if s.mod(T, C_LAG) == 0:
                        pe.wait_ge(w_landed, s.div(T, C_LAG) * 16 + 16)
                    if k == 0:
                        pe.wait_ge(act_z, s.count(1, plus=4, lag=C_LAG))
                    two = s.fixed and s.p == PAIRS and s.r > 0
                    if second_bank(s, C_LAG):
                        pe.wait_ge(dve_y, TILES)
                    wait(pe, act_o, s.count(1, plus=-1 if two else 0, lag=C_LAG))
                    for c in range(C):
                        last = te.matmul(ps_out(s, C_LAG)[:], w_sel[:, c, k * P:(k + 1) * P], zT[:, half, c, :],
                                         start=(c == 0), stop=(c == C - 1))
                    last.then_inc(pe_o, 1)
                if s.live():
                    pe.wait_ge(dve_xT, s.count(1, plus=1))
                    wait(pe, dve_y, s.count(1))
                    for c in range(C):
                        for i, (left, right) in enumerate(PARTS):
                            last = te.matmul(ps_h[:], xT[:, s.mod(2), left, c, :], w0T[:, right, c, :],
                                             start=(c + i == 0), stop=(c == C - 1 and i == 2))
                    last.then_inc(pe_h, 1)

            run_slots(pe, body)

            def rows(s):
                i = s.mod(RING)
                for t in range(T):
                    if t == 0:
                        pe.wait_ge(act_relu, C if s.r == 0 else s.count(C, plus=2 * C))
                    if s.r == 0 and t == T // 2:
                        pe.wait_ge(act_relu, 2 * C)
                    wait(pe, dve_y2, s.count(T, plus=t - 3))
                    for c in range(C):
                        last = te.transpose(ps_y[t % 4][:, c * P:(c + 1) * P], o_chunk(i, c)[:, t * P:(t + 1) * P], ident[:])
                    last.then_inc(pe_back, 1)

            run_steps(rows, 0)


_INS = ['x', 'adj', 'L0_gnn_mean_relation', 'L0_gnn_precision_relation', 'L0_gnn_W', 'L1_gnn_router_w',
        'L1_gnn_router_b', 'L1_gnn_expert_w', 'L1_gnn_bn_gamma', 'L1_gnn_bn_beta']


def kernel(**inputs):
    import numpy as _np
    import concourse.bacc as _bacc
    from concourse import mybir as _mybir
    from concourse.bass_utils import run_bass_kernel_spmd as _run

    nc = _bacc.Bacc("TRN2", target_bir_lowering=False, num_devices=1)
    arrays, args = {}, []
    for name in _INS:
        a = _np.ascontiguousarray(inputs[name])
        arrays[f"in_{name}_dram"] = a
        args.append(nc.dram_tensor(f"in_{name}_dram", a.shape, _mybir.dt.from_np(a.dtype), kind="ExternalInput").ap())
    nb, rows, width = inputs['x'].shape
    x1_spill = nc.dram_tensor("x1_spill", (nb, rows, width), F32, kind="Internal").ap()
    out_spill = nc.dram_tensor("out_spill", (nb, width, rows), F32, kind="Internal").ap()
    out = nc.dram_tensor("out_0_dram", (nb, rows, width), F32, kind="ExternalOutput").ap()
    gnn_program(nc, *args, x1_spill, out_spill, out)
    r = _run(nc, [arrays], core_ids=[0])
    return r.results[0]["out_0_dram"]
```
